# Optimizing a Trainium2 kernel written in Bass

```python
import numpy as np
import jax
import jax.numpy as jnp

def _softmax(x, axis=-1):
    return jax.nn.softmax(x, axis=axis)

def _gelu(x):
    return jax.nn.gelu(x, approximate=True)

def _silu(x):
    return jax.nn.silu(x)

def _sigmoid(x):
    return jax.nn.sigmoid(x)

def _layernorm(x, axis=-1, eps=1e-05):
    m = jnp.mean(x, axis=axis, keepdims=True)
    v = jnp.var(x, axis=axis, keepdims=True)
    return (x - m) / jnp.sqrt(v + eps)

def _scatter_add(tgt, idx, src, axis=0):
    return tgt.at[idx].add(src)

def _segment_sum(src, seg, n):
    return jax.ops.segment_sum(src, seg, n)
kernel_name = 'mk_hybrid_d1_jaxref_r8_749510'

def setup_inputs(seed: int=0):
    np.random.seed(seed)
    _w = jnp.asarray

    def _L0_attn_a_setup():
        import jax, jax.numpy as jnp
        import numpy as np
        B, N, D, H = (4, 256, 128, 8)
        HD = D // H
        TEMPER = 1.0
        LN_EPS = 1e-05

        def _leaky(x):
            return jnp.where(x > 0, x, 0.01 * x)
        key = jax.random.key(seed)
        ks = jax.random.split(key, 6)
        return {'h': jax.random.normal(ks[0], (B, N, D), dtype=jnp.float32), 'Wl': jax.random.normal(ks[1], (D, D), dtype=jnp.float32) * D ** (-0.5), 'Wr': jax.random.normal(ks[2], (D, D), dtype=jnp.float32) * D ** (-0.5), 'att_l': jax.random.normal(ks[3], (1, HD), dtype=jnp.float32) * HD ** (-0.5), 'att_r': jax.random.normal(ks[4], (1, HD), dtype=jnp.float32) * HD ** (-0.5), 'Wf': jax.random.normal(ks[5], (D, D), dtype=jnp.float32) * D ** (-0.5), 'ln_gamma': jnp.ones((D,), dtype=jnp.float32), 'ln_beta': jnp.zeros((D,), dtype=jnp.float32)}
    _L0_attn_a_in = _L0_attn_a_setup()

    def _L0_attn_b_setup():
        import jax, jax.numpy as jnp
        import numpy as np
        D_MODEL = 128
        N_HEADS = 16
        HEAD_DIM = D_MODEL // N_HEADS
        WINDOW = 128
        ROPE_BASE = 10000.0

        def _rope_cos_sin(T, dim, dtype):
            inv_freq = 1.0 / ROPE_BASE ** (jnp.arange(0, dim, 2, dtype=jnp.float32) / dim)
            freqs = jnp.arange(T, dtype=jnp.float32)[:, None] * inv_freq[None, :]
            emb = jnp.concatenate([freqs, freqs], axis=-1)
            return (jnp.cos(emb).astype(dtype), jnp.sin(emb).astype(dtype))

        def _rotate_half(x):
            h = x.shape[-1] // 2
            return jnp.concatenate([-x[..., h:], x[..., :h]], axis=-1)

        def _apply_rotary(x, cos, sin):
            c = cos[None, :, None, :]
            s = sin[None, :, None, :]
            return x * c + _rotate_half(x) * s
        key = jax.random.key(seed)
        ks = jax.random.split(key, 6)
        B, T = (2, 256)
        query = jax.random.normal(ks[0], (B, T, D_MODEL), dtype=jnp.float32)
        scale = 1.0 / np.sqrt(D_MODEL)
        Wq = jax.random.normal(ks[1], (D_MODEL, D_MODEL), dtype=jnp.float32) * scale
        Wk = jax.random.normal(ks[2], (D_MODEL, D_MODEL), dtype=jnp.float32) * scale
        Wv = jax.random.normal(ks[3], (D_MODEL, D_MODEL), dtype=jnp.float32) * scale
        Wo = jax.random.normal(ks[4], (D_MODEL, D_MODEL), dtype=jnp.float32) * scale
        bo = jax.random.normal(ks[5], (D_MODEL,), dtype=jnp.float32) * 0.01
        return {'query': query, 'Wq': Wq, 'Wk': Wk, 'Wv': Wv, 'Wo': Wo, 'bo': bo}
    _L0_attn_b_in = _L0_attn_b_setup()

    def _L0_ffn_setup():
        import jax, jax.numpy as jnp
        import numpy as np
        B, T, D, FF, E, TOP_K = (4, 256, 128, 512, 8, 2)
        key = jax.random.key(seed)
        k0, k1, k2, k3 = jax.random.split(key, 4)
        x = jax.random.normal(k0, (B, T, D), dtype=jnp.float32)
        router_w = jax.random.normal(k1, (E, D), dtype=jnp.float32) * D ** (-0.5)
        w1 = jax.random.normal(k2, (E, D, FF), dtype=jnp.float32) * D ** (-0.5)
        w2 = jax.random.normal(k3, (E, FF, D), dtype=jnp.float32) * FF ** (-0.5)
        return {'x': x, 'router_w': router_w, 'w1': w1, 'w2': w2}
    _L0_ffn_in = _L0_ffn_setup()
    _d = {'L0_attn_a_h': _L0_attn_a_in['h'], 'L0_attn_a_Wl': _L0_attn_a_in['Wl'], 'L0_attn_a_Wr': _L0_attn_a_in['Wr'], 'L0_attn_a_att_l': _L0_attn_a_in['att_l'], 'L0_attn_a_att_r': _L0_attn_a_in['att_r'], 'L0_attn_a_Wf': _L0_attn_a_in['Wf'], 'L0_attn_a_ln_gamma': _L0_attn_a_in['ln_gamma'], 'L0_attn_a_ln_beta': _L0_attn_a_in['ln_beta'], 'L0_attn_b_Wq': _L0_attn_b_in['Wq'], 'L0_attn_b_Wk': _L0_attn_b_in['Wk'], 'L0_attn_b_Wv': _L0_attn_b_in['Wv'], 'L0_attn_b_Wo': _L0_attn_b_in['Wo'], 'L0_attn_b_bo': _L0_attn_b_in['bo'], 'L0_ffn_router_w': _L0_ffn_in['router_w'], 'L0_ffn_w1': _L0_ffn_in['w1'], 'L0_ffn_w2': _L0_ffn_in['w2']}
    _x0 = _d['L0_attn_a_h']
    _d['L0_attn_a_h'] = jax.random.normal(jax.random.fold_in(jax.random.key(seed), 1), (8, 512, 128), dtype=_x0.dtype)
    del _x0
    return _d

def reference(L0_attn_a_h, L0_attn_a_Wl, L0_attn_a_Wr, L0_attn_a_att_l, L0_attn_a_att_r, L0_attn_a_Wf, L0_attn_a_ln_gamma, L0_attn_a_ln_beta, L0_attn_b_Wq, L0_attn_b_Wk, L0_attn_b_Wv, L0_attn_b_Wo, L0_attn_b_bo, L0_ffn_router_w, L0_ffn_w1, L0_ffn_w2):

    def _L0_attn_a_ref(h, Wl, Wr, att_l, att_r, Wf, ln_gamma, ln_beta):
        import jax, jax.numpy as jnp
        import numpy as np
        B, N, D, H = (4, 256, 128, 8)
        HD = D // H
        TEMPER = 1.0
        LN_EPS = 1e-05

        def _leaky(x):
            return jnp.where(x > 0, x, 0.01 * x)
        b, n, d = h.shape
        fl = (h @ Wl.T).reshape(b, n, H, HD).transpose(0, 2, 1, 3)
        fr = (h @ Wr.T).reshape(b, n, H, HD).transpose(0, 2, 1, 3)
        sl = jnp.einsum('bhnd,d->bhn', _leaky(fl), att_l[0])
        sr = jnp.einsum('bhnd,d->bhn', _leaky(fr), att_r[0])
        score = (sl[:, :, :, None] + sr[:, :, None, :]) / TEMPER
        p = jax.nn.softmax(score, axis=-1)
        ctx = jnp.einsum('bhnm,bhmd->bhnd', p, fr)
        h_sa = ctx.transpose(0, 2, 1, 3).reshape(b, n, d)
        fh = h_sa @ Wf.T
        y = h + fh
        mu = jnp.mean(y, axis=-1, keepdims=True)
        var = jnp.mean(jnp.square(y - mu), axis=-1, keepdims=True)
        return (y - mu) * jax.lax.rsqrt(var + LN_EPS) * ln_gamma + ln_beta

    def _L0_attn_b_ref(query, Wq, Wk, Wv, Wo, bo):
        import jax, jax.numpy as jnp
        import numpy as np
        D_MODEL = 128
        N_HEADS = 16
        HEAD_DIM = D_MODEL // N_HEADS
        WINDOW = 128
        ROPE_BASE = 10000.0

        def _rope_cos_sin(T, dim, dtype):
            inv_freq = 1.0 / ROPE_BASE ** (jnp.arange(0, dim, 2, dtype=jnp.float32) / dim)
            freqs = jnp.arange(T, dtype=jnp.float32)[:, None] * inv_freq[None, :]
            emb = jnp.concatenate([freqs, freqs], axis=-1)
            return (jnp.cos(emb).astype(dtype), jnp.sin(emb).astype(dtype))

        def _rotate_half(x):
            h = x.shape[-1] // 2
            return jnp.concatenate([-x[..., h:], x[..., :h]], axis=-1)

        def _apply_rotary(x, cos, sin):
            c = cos[None, :, None, :]
            s = sin[None, :, None, :]
            return x * c + _rotate_half(x) * s
        B, T, D = query.shape
        H, Dh = (N_HEADS, HEAD_DIM)
        sm_scale = Dh ** (-0.5)
        q = (query @ Wq.T).reshape(B, T, H, Dh)
        k = (query @ Wk.T).reshape(B, T, H, Dh)
        v = (query @ Wv.T).reshape(B, T, H, Dh)
        cos, sin = _rope_cos_sin(T, Dh, query.dtype)
        q = _apply_rotary(q, cos, sin)
        k = _apply_rotary(k, cos, sin)
        q = q.transpose(0, 2, 1, 3)
        k = k.transpose(0, 2, 1, 3)
        v = v.transpose(0, 2, 1, 3)
        scores = jnp.einsum('bhqd,bhkd->bhqk', q, k) * sm_scale
        i = jnp.arange(T)[:, None]
        j = jnp.arange(T)[None, :]
        mask = (j > i) | (j < i - (WINDOW - 1))
        scores = jnp.where(mask[None, None], jnp.float32(-jnp.inf), scores)
        attn = jax.nn.softmax(scores, axis=-1)
        out = jnp.einsum('bhqk,bhkd->bhqd', attn, v)
        out = out.transpose(0, 2, 1, 3).reshape(B, T, D)
        return out @ Wo.T + bo

    def _L0_ffn_ref(x, router_w, w1, w2):
        import jax, jax.numpy as jnp
        import numpy as np
        B, T, D, FF, E, TOP_K = (4, 256, 128, 512, 8, 2)
        b, t, d = x.shape
        e, k = (router_w.shape[0], TOP_K)
        xf = x.reshape(-1, d)
        n = xf.shape[0]
        logits = xf @ router_w.T
        topv, topi = jax.lax.top_k(logits, k)
        topw = jax.nn.softmax(topv.astype(jnp.float32), axis=-1).astype(x.dtype)
        idx_flat = topi.reshape(-1)
        w_flat = topw.reshape(-1)
        sort_idx = jnp.argsort(idx_flat)
        src = jnp.repeat(jnp.arange(n), k)
        rev = src[sort_idx]
        sw = w_flat[sort_idx]
        perm = xf[rev]
        chunks = perm.reshape(e, n * k // e, d)
        h = jax.nn.gelu(jnp.einsum('ecd,edf->ecf', chunks, w1), approximate=False)
        y = jnp.einsum('ecf,efd->ecd', h, w2).reshape(n * k, d)
        y = y * sw[:, None]
        out = jnp.zeros((n, d), dtype=x.dtype).at[rev].add(y)
        return out.reshape(b, t, d)
    x = L0_attn_a_h
    x = x + _L0_attn_a_ref(_layernorm(x, axis=-1), L0_attn_a_Wl, L0_attn_a_Wr, L0_attn_a_att_l, L0_attn_a_att_r, L0_attn_a_Wf, L0_attn_a_ln_gamma, L0_attn_a_ln_beta)
    x = x + _L0_ffn_ref(_layernorm(x, axis=-1), L0_ffn_router_w, L0_ffn_w1, L0_ffn_w2)
    x = x + _L0_attn_b_ref(_layernorm(x, axis=-1), L0_attn_b_Wq, L0_attn_b_Wk, L0_attn_b_Wv, L0_attn_b_Wo, L0_attn_b_bo)
    x = x + _L0_ffn_ref(_layernorm(x, axis=-1), L0_ffn_router_w, L0_ffn_w1, L0_ffn_w2)
    return x

_drawn_inputs = setup_inputs


def setup_inputs(seed=0):
    import zlib

    import numpy as np

    out = dict(_drawn_inputs(seed))
    spreads = {'L0_attn_a_ln_gamma': (1.0, 0.2), 'L0_attn_a_ln_beta': (0.0, 0.1)}
    factors = {}
    for name, (base, spread) in spreads.items():
        noise = np.random.default_rng([zlib.crc32(name.encode()), seed]).standard_normal(out[name].shape)
        drawn = base * np.exp(spread * noise) if base else spread * noise
        out[name] = jnp.asarray(drawn.astype(out[name].dtype))
    for name, factor in factors.items():
        out[name] = (out[name] * factor).astype(out[name].dtype)
    return out
```

```python
from contextlib import ExitStack, contextmanager

import numpy as np

import concourse.bass as bass
from concourse import mybir

P = 128
D = 128
B, N = 8, 512
TILES = B * N // P
GT = N // P
GROUPS = TILES // GT
HA = 8
HDA = D // HA
HB = 16
HDB = D // HB
E = 8
FF = 512
FC = FF // P
TOPK = 2
SLOTS = B * N * TOPK
SGT = 4
SG = SGT * P
SGROUPS = SLOTS // SG
ST = SLOTS // P
EPS = 1e-5
PARTS = 3
KROWS = PARTS * PARTS * HDB
KR1 = KROWS + 1
QUAD = 4
NQUAD = HB // QUAD
STEPS = GT * NQUAD
VW = HDB + 1
VC = 32
LANES = 4
NEG = -1.0e30

F32 = mybir.dt.float32
BF16 = mybir.dt.bfloat16
I32 = mybir.dt.int32
ALU = mybir.AluOpType
ACT = mybir.ActivationFunctionType
AX_X = mybir.AxisListType.X


class Chain:

    def __init__(self, eng, sem):
        self.eng, self.sem, self.base, self.n = eng, sem, 0, 0

    def did(self, ins):
        ins.then_inc(self.sem, 1)
        self.n += 1

    def settle(self):
        self.eng.wait_ge(self.sem, self.base + self.n)

    @contextmanager
    def turn(self, i, per):
        start, self.base = self.n, i * per
        yield
        assert self.n - start == per, (self.n - start, per)
        self.n = start

    def after(self, turns, per):
        self.base, self.n = 0, self.n + turns * per


def step_at(g, s, lag):
    q, r = divmod(s - lag, STEPS)
    return g + q, r, not isinstance(g, int) or 0 <= g + q < GROUPS


def tables():
    p, t, k = np.arange(P), np.arange(TILES), np.arange(TOPK)
    f = np.float32
    c = {}
    c["ident"] = np.eye(P, dtype=f)
    c["before"] = (p[:, None] < p[None, :]).astype(f)
    c["iota"] = np.tile(np.arange(P, dtype=f), (P, 1))
    c["entry"] = (TOPK * (P * t[None, None, :] + p[:, None, None]) + k[None, :, None]).astype(f).reshape(P, -1)
    c["order"] = np.tile((E - np.arange(E)).astype(f), (P, 1))
    c["head_of"] = (p[:, None] // HDA == np.arange(HA)[None, :]).astype(f)
    c["causal"] = (p[None, :] <= p[:, None]).astype(np.int32)
    c["causal_t"] = (p[:, None] <= p[None, :]).astype(f)
    inv = (f(1.0) / np.power(f(10000.0), np.arange(0, HDB, 2, dtype=f) / f(HDB))).astype(f)
    ang = np.arange(N, dtype=f)[:, None] * inv[None, :]
    ang = np.concatenate([ang, ang], -1).T.astype(f)
    sign = np.where(np.arange(HDB) < HDB // 2, -1.0, 1.0)[:, None]
    cos, sin = np.cos(ang.astype(np.float64)), np.sin(ang.astype(np.float64)) * sign
    for name, s in (("q", HDB ** -0.5), ("k", 1.0)):
        c["cos" + name] = np.repeat(cos * s, HB, 0).astype(f)
        c["sin" + name] = np.repeat(sin * s, HB, 0).astype(f)
    c["mark"] = np.full((1, HB * P), NEG, dtype=f)
    return c


def hybrid_block(nc, a, out):
    with ExitStack() as ctx:
        def sb(name, shape, dt=F32):
            return ctx.enter_context(nc.sbuf_tensor("sb_" + name, shape, dt))

        def sem(name):
            return ctx.enter_context(nc.semaphore(name))

        def sems(name, n):
            return [sem(f"{name}{k}") for k in range(n)]

        def psum(name, cols):
            return ctx.enter_context(nc.psum_tensor(name, [P, cols], F32))

        ps_s = [psum("ps_s0", 1024), psum("ps_s1", 1024)]
        bank = [ps_s[0][:, 0:512], ps_s[0][:, 512:1024], ps_s[1][:, 0:512], ps_s[1][:, 512:1024]]
        bank += [psum(f"bank{k}", 512)[:, :] for k in range(4, 8)]

        c_shapes = {"ident": P, "before": P, "iota": P, "entry": TOPK * TILES, "order": E, "head_of": HA,
                    "causal_t": P, "cosq": N, "sinq": N, "cosk": N, "sink": N}
        C = {k: sb("c_" + k, [P, w]) for k, w in c_shapes.items()}
        causal = sb("causal", [P, P], I32)
        W = {k: sb(k, [P, D]) for k in ("WrT", "WfT", "WqT", "WqrT", "WkT", "WkrT", "WvT", "WoT")}
        rwT = sb("rwT", [P, E])
        attr = sb("attr", [P, 1])
        gamma = sb("gamma", [P, D])
        beta = sb("beta", [P, D])
        bo = sb("bo", [P, D])
        neghalf = sb("neghalf", [P, TILES])
        zeros = sb("zeros", [P, 512])
        ones_bf = sb("ones_bf", [P, P], BF16)
        before_bf = sb("before_bf", [P, P], BF16)

        x = sb("x", [P, TILES, D])
        mean = sb("mean", [P, TILES])
        vareps = sb("vareps", [P, TILES])
        rstd = sb("rstd", [P, TILES])
        stat6 = sb("stat6", [P, GT, 6])
        mv = sb("mv", [P, GT, 2])
        xn = sb("xn", [P, 2, GT, D])
        xnT = sb("xnT", [P, 2, GT * P])
        upd = sb("upd", [P, 2, GT, D])

        h = sb("h", [P, TILES, D])
        leaky = sb("leaky", [P, 2, N])
        attpad = sb("attpad", [P, 2 * GROUPS * HA])
        attb = sb("attb", [P, 2, GROUPS * HA])
        HAB = GROUPS * HA
        nmax = sb("nmax", [P, 1])
        psum_row = sb("psum_row", [P, 1])
        prec = sb("prec", [P, 1])
        pa = sb("pa", [P, N])
        paT = sb("paT", [P, GT * HAB])
        GT_sb = sb("GT_sb", [P, HAB])
        ctxm = sb("ctxm", [P, HAB])
        ctxT = sb("ctxT", [P, GROUPS])
        fh = sb("fh", [P, GROUPS, D])

        lg = sb("lg", [P, TILES, E])
        top = sb("top", [P, TOPK, TILES])
        pick = sb("pick", [P, TILES, E])
        best = sb("best", [P, TILES])
        hot = sb("hot", [P, TOPK, TILES, E])
        wts = sb("wts", [P, TOPK, TILES])
        den = sb("den", [P, TILES])
        took = sb("took", [P, TILES * E], BF16)
        tot = sb("tot", [P, E, TILES])
        onesf = sb("onesf", [P, E * TILES])
        incl = sb("incl", [P, E, TILES])
        posf = sb("posf", [P, TILES, E])
        pos = sb("pos", [P, TOPK, TILES])
        pos_i = sb("pos_i", [P, 2, TOPK * TILES], I32)
        pos_hl = sb("pos_hl", [P, 2, TOPK * TILES])
        hot_lo = sb("hot_lo", [P, 2, TOPK, P])
        hot_hi = sb("hot_hi", [P, 2, TOPK, ST])
        entry_i = sb("entry_i", [P, ST], I32)
        token_i = sb("token_i", [P, ST], I32)

        w1b = sb("w1b", [P, 2, FF])
        w2b = sb("w2b", [P, 2, FC, D])
        tcol = sb("tcol", [P, 4, SGT], I32)
        ecol = sb("ecol", [P, 4, SGT], I32)
        xg = sb("xg", [P, 4, SGT, D])
        xs = sb("xs", [P, 2, SG])
        hid = sb("hid", [P, FC, SG])
        ys = sb("ys", [P, 4, SGT, D])
        yb = sb("yb", [P, 2, GT, TOPK * D])

        rot = hid[:].rearrange("p (m c) n -> p m c n", m=2)
        qk = sb("qk", [P, 2, N])
        part = sb("part", [P, 2, PARTS, N], BF16)
        vE = sb("vE", [P, TILES + 1, HB * VW])
        qb = h[:].rearrange("p t d -> p (t d)").bitcast(BF16).rearrange("p (j c) -> p j c", j=GT)
        kb = sb("kb", [P, GT + 1, HB * P], BF16)
        nm = sb("nm", [P, 2, QUAD])
        pb = yb[:].rearrange("p u t c -> p (u t c)").rearrange("p (b k j) -> p b k j", b=LANES, j=P)
        pT = xg[:].rearrange("p u k q -> p u (k q)")
        pTc = ys[:].rearrange("p u k q -> p u (k q)")
        vp = sb("vp", [P, 2, HB, VC])
        vd = sb("vd", [P, 2, HB, VC])
        oS = sb("oS", [P, 2, NQUAD * P])
        rden = sb("rden", [P, 2, HB])
        ob = sb("ob", [P, 2, D])
        oT = sb("oT", [P, 2, P])
        markf = sb("markf", [P, 1])

        def dram(name, shape, dt=F32):
            return nc.dram_tensor(name, shape, dt).ap()

        xn_dram = [dram(f"xn_dram{r}", (B * N, D)) for r in range(2)]
        y_dram = [dram(f"y_dram{r}", (SLOTS, D)) for r in range(2)]
        q_dram = dram("q_dram", (PARTS, TILES, HDB, HB, P), BF16)
        k_dram = dram("k_dram", (PARTS, TILES, HDB, HB, P), BF16)

        const_in = sem("const_in")
        x_in = sems("x_in", 2)
        consts_made = sem("consts_made")
        pool_chain = sem("pool_chain")
        act_chain = sem("act_chain")
        dve_chain = [sem(f"dve_chain{k}") for k in range(12)]
        spacer = {e: sem("spacer_" + e) for e in ("pool", "act", "dve")}
        stats_done = sems("stats_done", 5)
        rstd_ready = sems("rstd_ready", 5)
        xn_ready = sems("xn_ready", 4)
        xn_saved = sems("xn_saved", 4)
        xn_out = {r: sem(f"xn_out{r}") for r in (1, 3)}
        xT_ready = sems("xT_ready", 4)
        xnT_ready = sems("xnT_ready", 4)

        fr_ready = sem("fr_ready")
        fr_scaled = sem("fr_scaled")
        fills = sem("fills")
        leaky_ready = sem("leaky_ready")
        sr_done = sem("sr_done")
        attb_ready = sem("attb_ready")
        a_pe = sem("a_pe")
        a_act = sem("a_act")
        a_dve = sem("a_dve")
        beta_added = sem("beta_added")

        lg_ready = {r: sem(f"lg_ready{r}") for r in (1, 3)}
        lg_read = {r: sem(f"lg_read{r}") for r in (1, 3)}
        took_ready = {r: sem(f"took_ready{r}") for r in (1, 3)}
        rank_ready = {r: sem(f"rank_ready{r}") for r in (1, 3)}
        hot_ready = {r: sem(f"hot_ready{r}") for r in (1, 3)}
        hot_used = {r: sem(f"hot_used{r}") for r in (1, 3)}
        wd_ready = {r: sem(f"wd_ready{r}") for r in (1, 3)}
        we_ready = {r: sem(f"we_ready{r}") for r in (1, 3)}
        index_ready = {r: sem(f"index_ready{r}") for r in (1, 3)}
        w_in = {r: sems(f"w_in{r}_", 2) for r in (1, 3)}
        g_in = {r: sems(f"g_in{r}_", 4) for r in (1, 3)}
        xgT_ready = {r: sem(f"xgT_ready{r}") for r in (1, 3)}
        xs_ready = {r: sem(f"xs_ready{r}") for r in (1, 3)}
        h_ready = {r: sem(f"h_ready{r}") for r in (1, 3)}
        gelu_done = {r: sem(f"gelu_done{r}") for r in (1, 3)}
        y_ready = {r: sem(f"y_ready{r}") for r in (1, 3)}
        ys_ready = {r: sem(f"ys_ready{r}") for r in (1, 3)}
        ys_free = {r: sem(f"ys_free{r}") for r in (1, 3)}
        y_out = {r: sems(f"y_out{r}_", 4) for r in (1, 3)}
        yb_in = {r: sems(f"yb_in{r}_", 2) for r in (1, 3)}
        x_done = {r: sem(f"x_done{r}") for r in (1, 3)}

        proj_ready = sem("proj_ready")
        rot_ready = sem("rot_ready")
        qk_ready = sem("qk_ready")
        part1 = sem("part1")
        rest1 = sem("rest1")
        part2 = sem("part2")
        part3 = sem("part3")
        parts_out = sem("parts_out")
        parts_free = sem("parts_free")
        v_ready = sem("v_ready")
        v_copied = sem("v_copied")
        bo_added = sem("bo_added")
        mark_in = sem("mark_in")
        mark_made = sem("mark_made")
        mark_ready = sem("mark_ready")
        qk_in = sems("qk_in", GT)
        s_ready = sem("s_ready")
        merged = sem("merged")
        rden_ready = sem("rden_ready")
        nm_ready = sem("nm_ready")
        p_ready = sem("p_ready")
        pT_ready = sem("pT_ready")
        pT_copied = sem("pT_copied")
        pTc_ready = sem("pTc_ready")
        vt_ready = sem("vt_ready")
        pv_done = sem("pv_done")
        oS_ready = sem("oS_ready")
        oq_ready = sem("oq_ready")
        o_ready = sem("o_ready")
        x_added = sem("x_added")
        oT_ready = sem("oT_ready")
        oT_copied = sem("oT_copied")
        wo_done = sem("wo_done")
        out_done = sem("out_done")

        xnT_read = {0: fr_ready, 1: lg_ready[1], 2: v_ready, 3: lg_ready[3]}

        block = ctx.enter_context(nc.Block())
        NCONST = len(C) + 1 + len(W) + 5

        def tile(t):
            return bass.ds(t, 1)

        TURN_LAG, WEIGH_LAG = 2, 5
        TAKE_LAG, TURN_RES_LAG, NORM_LAG, OT_LAG, PROJ_LAG, ADD_LAG = 9, 9, 10, 11, 12, 12

        def slots(eng, slot):
            for s in range(STEPS):
                slot(0, s)
            with eng.Fori(1, GROUPS) as g:
                for s in range(STEPS):
                    slot(g, s)
            for s in range(ADD_LAG + 1):
                slot(GROUPS, s)

        def flat(ap):
            return ap.rearrange("p a d -> p (a d)")

        @block.sync
        def _(sp):
            xt = a["x"].rearrange("(t p) d -> p t d", p=P)
            for half in range(2):
                s = slice(half * TILES // 2, (half + 1) * TILES // 2)
                sp.dma_start(x[:, s, :], xt[:, s, :]).then_inc(x_in[half], 16)
            for k in C:
                sp.dma_start(C[k][:], a["c_" + k]).then_inc(const_in, 16)
            sp.dma_start(causal[:], a["c_causal"]).then_inc(const_in, 16)
            for k in W:
                sp.dma_start(W[k][:], a[k]).then_inc(const_in, 16)
            sp.dma_start(rwT[:], a["rwT"]).then_inc(const_in, 16)
            sp.dma_start(attr[:], a["attr"]).then_inc(const_in, 16)
            for dst, k in ((gamma, "gamma"), (beta, "beta"), (bo, "bo")):
                sp.dma_start(dst[:], a[k].broadcast_to([P, D])).then_inc(const_in, 16)

            def ffn(r):
                n = r // 2
                sp.sem_inc(xn_saved[r], 2)
                rows = xn_dram[n].rearrange("(t p) d -> p t d", p=P)
                with sp.Fori(0, GROUPS // 2) as i:
                    for u in range(2):
                        g = i * 2 + u
                        sp.wait_ge(xn_ready[r], g + 1)
                        sp.dma_start(rows[:, bass.ds(g * GT, GT), :], xn[:, u]).then_inc(xn_out[r], 16)
                        sp.wait_ge(xn_out[r], g * 16 + 16)
                        sp.sem_inc(xn_saved[r], 1)
                sp.sem_inc(ys_free[r], 4)
                w1r = a["w1"].rearrange("e d f -> d e f")
                w2r = a["w2"].rearrange("e (c f) d -> f e c d", f=P)

                def load_expert(e, u):
                    sp.dma_start(w1b[:, u], flat(w1r[:, tile(e), :])).then_inc(w_in[r][u], 16)
                    sp.dma_start(w2b[:, u], w2r[:, tile(e)].rearrange("f e c d -> f (e c) d")).then_inc(w_in[r][u], 16)

                for u in range(2):
                    load_expert(u, u)
                with sp.Fori(0, SGROUPS // 4) as i:
                    for k in range(4):
                        sp.wait_ge(y_out[r][k], i * (16 * SGT) + 16 * SGT)
                        sp.sem_inc(ys_free[r], 1)
                        if k % 2 == 1:
                            sp.wait_ge(y_ready[r], i * 4 + k + 1)
                            load_expert((i * 2 + 2 + k // 2) % E, k // 2)
                for u in range(2):
                    sp.wait_ge(w_in[r][u], 32 * (E // 2 + 1))
                yr = y_dram[n].rearrange("(t p k) d -> p t (k d)", p=P, k=TOPK)
                with sp.Fori(0, GROUPS // 2) as i:
                    for u in range(2):
                        g = i * 2 + u
                        sp.wait_ge(x_done[r], g + 1)
                        sp.dma_start(yb[:, u], yr[:, bass.ds(g * GT, GT), :]).then_inc(yb_in[r][u], 16)

            ffn(1)

            sp.sem_inc(parts_free, 1)
            src = (q_dram, k_dram)
            with sp.Fori(0, GROUPS) as g:
                sp.wait_ge(part3, g * 2 + 4)
                for m in range(2):
                    for c in range(PARTS):
                        dst = src[m][c].rearrange("t d h n -> (d h) t n")[:, bass.ds(g * GT, GT), :]
                        sp.dma_start(dst, part[:, m, c, :].rearrange("p (t n) -> p t n", n=P)).then_inc(parts_out, 16)
                sp.wait_ge(parts_out, g * (16 * 2 * PARTS) + 16 * 2 * PARTS)
                sp.sem_inc(parts_free, 1)

            def load_qk(g, j):
                t = g * GT + j
                for c in range(PARTS):
                    rows = slice(c * PARTS * HDB, (c + 1) * PARTS * HDB)
                    qsrc = q_dram[:, tile(t)].rearrange("a t d h n -> a (t d) (h n)")
                    ksrc = k_dram[c:c + 1, tile(t)].rearrange("c t d h n -> c (t d) (h n)")
                    sp.dma_start(qb[rows, j], qsrc).then_inc(qk_in[j], 16)
                    sp.dma_start(kb[rows, j + 1], ksrc.broadcast_to([PARTS, HDB, HB * P])).then_inc(qk_in[j], 16)

            sp.wait_ge(mark_ready, 1)
            for j in range(GT):
                load_qk(0, j)
            with sp.Fori(1, GROUPS) as g:
                for j in range(GT):
                    sp.wait_ge(s_ready, g * STEPS - STEPS + min(j + 2, GT) * NQUAD)
                    load_qk(g, j)

            ffn(3)
            ot = out.rearrange("(t p) d -> p t d", p=P)
            with sp.Fori(0, GROUPS) as g:
                sp.wait_ge(x_done[3], g + 3)
                sp.dma_start(ot[:, bass.ds(g * GT, GT), :], x[:, bass.ds(g * GT, GT), :]).then_inc(out_done, 16)
            sp.wait_ge(out_done, 16 * GROUPS)

        @block.gpsimd
        def _(pool):
            ch = Chain(pool, pool_chain)

            def hold(s, value):
                pool.wait_ge(s, value)
                pool.sem_inc(spacer["pool"], 1)

            pool.memset(neghalf[:], -0.5).then_inc(consts_made, 1)
            pool.memset(zeros[:], 0.0).then_inc(consts_made, 1)
            pool.memset(ones_bf[:], 1.0).then_inc(consts_made, 1)
            pool.memset(onesf[:], 1.0).then_inc(consts_made, 1)
            pool.memset(attpad[:], 0.0).then_inc(consts_made, 1)

            def make_rstd(r):
                pool.wait_ge(stats_done[r], GROUPS)
                pool.tensor_tensor(rstd[:], vareps[:], neghalf[:], ALU.pow).then_inc(rstd_ready[r], 1)

            pool.wait_ge(consts_made, 7)
            pool.wait_ge(const_in, 16 * NCONST)
            make_rstd(0)
            pool.sem_inc(xn_saved[0], 2)
            with pool.Fori(0, GROUPS // 2) as i:
                for u in range(2):
                    g = i * 2 + u
                    hold(sr_done, g + 1)
                    pool.tensor_copy(attb[:, u], attpad[:, bass.ds(GROUPS * HA - HA - g * HA, GROUPS * HA)])\
                        .then_inc(attb_ready, 1)
                    hold(xn_ready[0], g + 1)
                    pool.tensor_copy(h[:, bass.ds(g * GT, GT), :], xn[:, u]).then_inc(xn_saved[0], 1)
            pool.tensor_tensor(x[:], x[:], beta[:].unsqueeze(1).broadcast_to([P, TILES, D]), ALU.add)\
                .then_inc(beta_added, 1)
            make_rstd(4)

            def ffn(r):
                n = r // 2
                make_rstd(r)
                if r == 1:
                    pool.memset(vE[:], 1.0).then_inc(fills, 1)
                    pool.memset(qb, 1.0).then_inc(fills, 1)
                    pool.memset(kb[:], 0.0).then_inc(fills, 1)
                    pool.memset(vp[:], 0.0).then_inc(fills, 1)
                    pool.memset(vd[:], 0.0).then_inc(fills, 1)
                pool.wait_ge(index_ready[r], 1)

                def columns(G, k):
                    ch.did(pool.tensor_copy(tcol[:, k], token_i[:, bass.ds(G * SGT, SGT)]))
                    ch.did(pool.tensor_copy(ecol[:, k], entry_i[:, bass.ds(G * SGT, SGT)]))

                def gather(k):
                    for j in range(SGT):
                        pool.indirect_dma_start(xg[:, k, j, :], None, xn_dram[n],
                                                bass.IndirectOffsetOnAxis(ap=tcol[:, k, j:j + 1], axis=0))\
                            .then_inc(g_in[r][k], 16)

                def scatter(k):
                    for j in range(SGT):
                        pool.indirect_dma_start(y_dram[n], bass.IndirectOffsetOnAxis(ap=ecol[:, k, j:j + 1], axis=0),
                                                ys[:, k, j, :], None).then_inc(y_out[r][k], 16)

                def settle_hold():
                    ch.settle()
                    pool.sem_inc(spacer["pool"], 1)

                pool.wait_ge(xn_saved[r], GROUPS + 2)
                for k in range(2):
                    columns(k, k)
                ch.settle()
                for k in range(2):
                    gather(k)

                def turn(i, last):
                    for k in range(4):
                        G = i * 4 + k
                        if not (last and k >= 2):
                            k2 = (k + 2) % 4
                            hold(xgT_ready[r], G + 3)
                            hold(ys_free[r], G + 3)
                            columns(G + 2, k2)
                            settle_hold()
                            gather(k2)
                        hold(ys_ready[r], G + 1)
                        scatter(k)

                turns = SGROUPS // 4
                with pool.Fori(0, turns - 1) as i:
                    with ch.turn(i, 8):
                        turn(i, False)
                ch.after(turns - 1, 8)
                turn(turns - 1, True)
                for k in range(4):
                    pool.wait_ge(y_out[r][k], 16 * SGT * turns)
            ffn(1)

            make_rstd(2)
            pool.sem_inc(part3, 2)
            with pool.Fori(0, GROUPS) as g:
                for m in range(2):
                    pool.wait_ge(part1, g * 2 + m + 1)
                    pool.tensor_tensor(qk[:, m], qk[:, m], part[:, m, 0], ALU.subtract).then_inc(rest1, 1)
                for m in range(2):
                    pool.wait_ge(part2, g * 2 + m + 1)
                    pool.tensor_tensor(part[:, m, 2], qk[:, m], part[:, m, 1], ALU.subtract).then_inc(part3, 1)
            pool.wait_ge(xn_ready[2], GROUPS)
            pool.tensor_tensor(x[:], x[:], bo[:].unsqueeze(1).broadcast_to([P, TILES, D]), ALU.add)\
                .then_inc(bo_added, 1)
            pool.wait_ge(v_copied, GROUPS)
            def heads(v):
                return v.rearrange("p t (h c) -> p (t h) c", c=VW)

            def values(g, j):
                t = g * GT + j
                hold(pv_done, (t + 1) * NQUAD)
                pool.tensor_copy(vp[:, j % 2, :, 0:VW], heads(vE[:, tile(t), :])).then_inc(vt_ready, 1)
                pool.tensor_tensor(vd[:, j % 2, :, 0:VW], heads(vE[:, tile(t + 1), :]), heads(vE[:, tile(t), :]),
                                   ALU.subtract).then_inc(vt_ready, 1)

            with pool.Fori(0, GROUPS) as g:
                for s in range(STEPS):
                    if s % NQUAD == 0:
                        values(g, s // NQUAD)
                    pool.wait_ge(pT_copied, g * STEPS + s + 1)
                    pool.tensor_tensor(pTc[:, s % LANES].rearrange("p (k q) -> p k q", q=P),
                                       pT[:, s % LANES].rearrange("p (k q) -> p k q", q=P),
                                       C["causal_t"][:].unsqueeze(1).broadcast_to([P, QUAD, P]), ALU.mult)\
                        .then_inc(pTc_ready, 1)

            ffn(3)

        @block.scalar
        def _(act):
            ch = Chain(act, act_chain)

            def hold(s, value):
                act.wait_ge(s, value)
                act.sem_inc(spacer["act"], 1)

            def copy_xT(r, g, u):
                act.wait_ge(xnT_read[r], g + 1)
                act.wait_ge(xT_ready[r], g + 3)
                act.activation(xnT[:, u], bank[u], ACT.Copy).then_inc(xnT_ready[r], 1)

            with act.Fori(0, GROUPS // 2) as i:
                for u in range(2):
                    copy_xT(0, i * 2 + u, u)
            act.wait_ge(a_dve, 1)
            act.activation(pa[0:HAB, :], bank[4][0:HAB, :], ACT.Exp, bias=nmax[0:HAB, :],
                           accum_out=psum_row[0:HAB, :]).then_inc(a_act, 1)
            act.wait_ge(a_pe, 1)
            act.activation(paT[:], bank[5][:, 0:GT * HAB], ACT.Copy).then_inc(a_act, 1)
            act.wait_ge(a_pe, 2)
            act.activation(GT_sb[:], bank[6][:, 0:HAB], ACT.Copy).then_inc(a_act, 1)
            for b in range(2):
                act.wait_ge(a_pe, 4 + b)
                act.activation(fh[:, b * GT:(b + 1) * GT, :].rearrange("p a d -> p (a d)"), bank[b], ACT.Copy)\
                    .then_inc(a_act, 1)

            def ffn(r):
                with act.Fori(0, GROUPS // 2) as i:
                    for u in range(2):
                        copy_xT(r, i * 2 + u, u)
                act.wait_ge(wd_ready[r], 1)
                act.activation(wts[:, 1], wts[:, 1], ACT.Exp).then_inc(we_ready[r], 1)
                with act.Fori(0, SGROUPS) as G:
                    for c in range(FC):
                        act.wait_ge(h_ready[r], G * FC + (c + 1))
                        act.activation(hid[:, c], bank[1 + c], ACT.Gelu).then_inc(gelu_done[r], 1)
            ffn(1)

            act.dma_start(markf[0:1, :], a["c_mark"][:, 0:1]).then_inc(mark_in, 16)
            act.wait_ge(mark_in, 16)
            act.wait_ge(fills, 5)
            act.activation(pT[0:1, 0, :].bitcast(BF16)[:, 0:P], zeros[0:1, 0:P], ACT.Identity, bias=markf[0:1, :])\
                .then_inc(mark_made, 1)
            act.wait_ge(mark_made, 1)
            for hh in range(HB):
                act.dma_start(kb[KROWS:KR1, 0, hh * P:(hh + 1) * P], pT[0:1, 0, :].bitcast(BF16)[:, 0:P]).then_inc(mark_in, 16)
            act.wait_ge(mark_in, 16 * (HB + 1))
            act.sem_inc(mark_ready, 1)

            with act.Fori(0, GROUPS // 2) as i:
                for u in range(2):
                    g = i * 2 + u
                    copy_xT(2, g, u)
                    hold(v_ready, g + 3)
                    act.activation(
                        vE[:, bass.ds(g * GT + 1, GT), :].rearrange("p t (h c) -> p (t h) c", c=VW)[:, :, 0:HDB],
                        bank[6 + u].rearrange("p (th c) -> p th c", c=HDB), ACT.Copy).then_inc(v_copied, 1)
                    for m in range(2):
                        act.wait_ge(parts_free, g + 1)
                        act.wait_ge(qk_ready, g * 2 + m + 1)
                        act.activation(part[:, m, 0], qk[:, m], ACT.Copy).then_inc(part1, 1)
                    for m in range(2):
                        act.wait_ge(rest1, g * 2 + m + 1)
                        act.activation(part[:, m, 1], qk[:, m], ACT.Copy).then_inc(part2, 1)
            def slot(g, s):
                g0, s0, there = step_at(g, s, 0)
                if there:
                    act.wait_ge(nm_ready, g0 * STEPS + s0 + 1)
                    for k in range(QUAD):
                        ins = act.activation(pb[:, s0 % LANES, k, :], ps_s[s0 % 2][:, 2 * k * P:(2 * k + 1) * P], ACT.Exp,
                                             bias=nm[:, s0 % 2, k:k + 1])
                    ins.then_inc(p_ready, 1)
                g0, s0, there = step_at(g, s, TURN_LAG)
                if there:
                    act.wait_ge(pT_ready, g0 * STEPS + s0 + 1)
                    act.activation(pT[:, s0 % LANES], bank[4 + s0 % 2], ACT.Copy).then_inc(pT_copied, 1)
                g0, s0, there = step_at(g, s, OT_LAG)
                if there and s0 % NQUAD == 0:
                    j = s0 // NQUAD
                    act.wait_ge(oT_ready, g0 * GT + j + 1)
                    act.activation(oT[:, j % 2], bank[6 + j % 2][:, 0:P], ACT.Copy).then_inc(oT_copied, 1)

            slots(act, slot)
            ffn(3)

        @block.vector
        def _(dve):
            chains = iter(dve_chain)

            def new_chain():
                return Chain(dve, next(chains))

            def hold(s, value):
                dve.wait_ge(s, value)
                dve.sem_inc(spacer["dve"], 1)

            def stats(ch, src, g, done):
                for j in range(GT):
                    ch.did(dve.bn_stats(stat6[:, j, :], flat(src[:, tile(g * GT + j), :])))
                ch.settle()
                dve.sem_inc(spacer["dve"], 1)
                for j in range(GT):
                    ch.did(dve.bn_aggr(mv[:, j, :], stat6[:, j, :]))
                ch.settle()
                dve.sem_inc(spacer["dve"], 1)
                ch.did(dve.tensor_copy(mean[:, bass.ds(g * GT, GT)], mv[:, :, 0]))
                dve.tensor_scalar(vareps[:, bass.ds(g * GT, GT)], mv[:, :, 1], EPS, None, ALU.add).then_inc(done, 1)

            def norm(r, extra):
                dve.wait_ge(rstd_ready[r], 1)
                with dve.Fori(0, GROUPS // 2) as i:
                    for u in range(2):
                        g = i * 2 + u
                        dve.wait_ge(xT_ready[r], g + 1)
                        if r != 2:
                            dve.wait_ge(xn_saved[r], g + 1)
                        for j in range(GT):
                            t = g * GT + j
                            ins = dve.tensor_scalar(xn[:, u, j, :], flat(x[:, tile(t), :]), mean[:, tile(t)],
                                                    rstd[:, tile(t)], ALU.subtract, ALU.mult)
                        ins.then_inc(xn_ready[r], 1)
                        if extra:
                            extra(i, g, u)

            dve.wait_ge(consts_made, 5)
            dve.wait_ge(const_in, 16 * NCONST)
            dve.tensor_copy(before_bf[:], C["before"][:]).then_inc(consts_made, 1)
            dve.tensor_scalar(attpad[:, GROUPS * HA - HA:GROUPS * HA], C["head_of"][:], attr[:, 0:1], None, ALU.mult)\
                .then_inc(consts_made, 1)

            ch = new_chain()
            for half in range(2):
                dve.wait_ge(x_in[half], 16)
                with dve.Fori(half * GROUPS // 2, (half + 1) * GROUPS // 2) as g:
                    with ch.turn(g, 9):
                        stats(ch, x, g, stats_done[0])
            ch.after(GROUPS, 9)

            def leaky_part(i, g, u):
                dve.wait_ge(sr_done, g + 1)
                dve.wait_ge(fr_ready, g + 3)
                dve.tensor_scalar(leaky[:, u], bank[2 + u], 0.01, None, ALU.mult).then_inc(fr_scaled, 1)
                dve.wait_ge(fr_scaled, g + 1)
                dve.tensor_tensor(leaky[:, u], leaky[:, u], bank[2 + u], ALU.max).then_inc(leaky_ready, 1)

            norm(0, leaky_part)
            dve.wait_ge(sr_done, GROUPS + 2)
            dve.tensor_reduce(nmax[0:HAB, :], bank[4][0:HAB, :], AX_X, ALU.max, negate=True).then_inc(a_dve, 1)
            dve.wait_ge(a_act, 1)
            ch.did(dve.reciprocal(prec[0:HAB, :], psum_row[0:HAB, :]))
            ch.settle()
            dve.tensor_scalar(pa[0:HAB, :], pa[0:HAB, :], prec[0:HAB, 0:1], None, ALU.mult).then_inc(a_dve, 1)
            dve.wait_ge(a_pe, 3)
            ch.did(dve.tensor_tensor(ctxm[:].rearrange("p (b h) -> p b h", h=HA),
                                     bank[7][:, 0:HAB].rearrange("p (b h) -> p b h", h=HA),
                                     C["head_of"][:].unsqueeze(1).broadcast_to([P, GROUPS, HA]), ALU.mult))
            ch.settle()
            dve.tensor_reduce(ctxT[:], ctxm[:].rearrange("p (b h) -> p b h", h=HA), AX_X, ALU.add).then_inc(a_dve, 1)
            dve.wait_ge(a_act, 5)
            dve.wait_ge(xn_saved[0], GROUPS + 2)
            ch = new_chain()
            with dve.Fori(0, GROUPS) as g:
                with ch.turn(g, 10):
                    hg = h[:, bass.ds(g * GT, GT), :]
                    ch.did(dve.tensor_tensor(hg, hg, fh[:, tile(g), :].broadcast_to([P, GT, D]), ALU.add))
                    ch.settle()
                    dve.sem_inc(spacer["dve"], 1)
                    stats(ch, h, g, stats_done[4])
            dve.wait_ge(rstd_ready[4], 1)
            dve.wait_ge(beta_added, 1)
            ch = new_chain()
            with dve.Fori(0, GROUPS // 2) as i:
                with ch.turn(i, 16):
                    for u in range(2):
                        g = i * 2 + u
                        for j in range(GT):
                            t = g * GT + j
                            ch.did(dve.scalar_tensor_tensor(upd[:, u, j, :], flat(h[:, tile(t), :]), mean[:, tile(t)],
                                                            gamma[:], ALU.subtract, ALU.mult))
                        ch.settle()
                        for j in range(GT):
                            t = g * GT + j
                            ch.did(dve.scalar_tensor_tensor(flat(x[:, tile(t), :]), upd[:, u, j, :], rstd[:, tile(t)],
                                                            flat(x[:, tile(t), :]), ALU.mult, ALU.add))
            ch.after(GROUPS // 2, 16)
            ch.settle()

            def all_stats(r):
                ch = new_chain()
                with dve.Fori(0, GROUPS) as g:
                    with ch.turn(g, 9):
                        stats(ch, x, g, stats_done[r])
                ch.after(GROUPS, 9)
                ch.settle()

            def bc(ap, n):
                return ap.unsqueeze(2).broadcast_to([P, TILES, n])

            def order():
                return C["order"][:].unsqueeze(1).broadcast_to([P, TILES, E])

            def ffn(r):
                all_stats(r)

                def keep_logits(i, g, u):
                    dve.wait_ge(lg_ready[r], g + 3)
                    dve.tensor_scalar(lg[:, bass.ds(g * GT, GT), :],
                                      bank[2 + u][:, 0:GT * E].rearrange("p (t e) -> p t e", e=E), 1.0, None, ALU.mult)\
                        .then_inc(lg_read[r], 1)

                norm(r, keep_logits)
                ch = new_chain()
                dve.wait_ge(lg_read[r], GROUPS + 2)
                for c in range(TOPK):
                    ch.did(dve.tensor_reduce(top[:, c], lg[:], AX_X, ALU.max))
                    ch.settle()
                    ch.did(dve.tensor_tensor(pick[:], lg[:], bc(top[:, c], E), ALU.is_equal))
                    ch.settle()
                    ch.did(dve.tensor_tensor(pick[:], pick[:], order(), ALU.mult))
                    ch.settle()
                    ch.did(dve.tensor_reduce(best[:], pick[:], AX_X, ALU.max))
                    ch.settle()
                    ch.did(dve.tensor_tensor(hot[:, c], order(), bc(best[:], E), ALU.is_equal))
                    ch.settle()
                    if c == 0:
                        ch.did(dve.scalar_tensor_tensor(lg[:], hot[:, 0], -3.0e38, lg[:], ALU.mult, ALU.add))
                        ch.settle()
                dve.tensor_tensor(took[:].rearrange("p (t e) -> p t e", e=E), hot[:, 0], hot[:, 1], ALU.add)\
                    .then_inc(took_ready[r], 1)
                dve.tensor_tensor(wts[:, 1], top[:, 1], top[:, 0], ALU.subtract).then_inc(wd_ready[r], 1)
                dve.wait_ge(rank_ready[r], 1)
                ch.did(dve.tensor_copy(tot[:], bank[5][:, 0:TILES * E].rearrange("p (t e) -> p e t", e=E)))
                ch.settle()
                ch.did(dve.tensor_tensor_scan(incl[:].rearrange("p e t -> p (e t)"), onesf[:],
                                              tot[:].rearrange("p e t -> p (e t)"), 0.0, ALU.mult, ALU.add))
                ch.settle()
                ch.did(dve.tensor_tensor(incl[:], incl[:], tot[:], ALU.subtract))
                ch.settle()
                ch.did(dve.tensor_tensor(posf[:], bank[4][:, 0:TILES * E].rearrange("p (t e) -> p t e", e=E),
                                         incl[:].rearrange("p e t -> p t e"), ALU.add))
                ch.settle()
                for c in range(TOPK):
                    ch.did(dve.tensor_tensor(pick[:], hot[:, c], posf[:], ALU.mult))
                    ch.settle()
                    ch.did(dve.tensor_reduce(pos[:, c], pick[:], AX_X, ALU.add))
                    ch.settle()
                ch.did(dve.tensor_copy(pos_i[:, 0], pos[:].rearrange("p k t -> p (k t)")))
                ch.settle()
                ch.did(dve.tensor_scalar(pos_i[:, 1], pos_i[:, 0], P - 1, None, ALU.bitwise_and))
                ch.settle()
                ch.did(dve.tensor_scalar(pos_i[:, 0], pos_i[:, 0], 7, None, ALU.logical_shift_right))
                ch.settle()
                ch.did(dve.tensor_copy(pos_hl[:], pos_i[:]))
                ch.settle()
                dve.wait_ge(we_ready[r], 1)
                ch.did(dve.tensor_scalar(den[:], wts[:, 1], 1.0, None, ALU.add))
                ch.settle()
                ch.did(dve.reciprocal(wts[:, 0], den[:]))
                ch.settle()
                ch.did(dve.tensor_tensor(wts[:, 1], wts[:, 1], wts[:, 0], ALU.mult))
                with dve.Fori(0, TILES // 2) as i:
                    for u in range(2):
                        t = i * 2 + u
                        dve.wait_ge(hot_used[r], t + 1)
                        for c in range(TOPK):
                            col = bass.ds(c * TILES + t, 1)
                            dve.tensor_scalar(hot_lo[:, u, c], C["iota"][:], pos_hl[:, 1, col], None, ALU.is_equal)
                            ins = dve.tensor_scalar(hot_hi[:, u, c], C["iota"][:, 0:ST], pos_hl[:, 0, col],
                                                    C["entry"][:, col], ALU.is_equal, ALU.mult)
                        ins.then_inc(hot_ready[r], 1)
                dve.wait_ge(hot_used[r], TILES + 2)
                ch.did(dve.tensor_copy(entry_i[:], bank[6][:, 0:ST]))
                ch.settle()
                dve.tensor_scalar(token_i[:], entry_i[:], 1, None, ALU.logical_shift_right).then_inc(index_ready[r], 1)

                def copy_x(G, u):
                    dve.wait_ge(xgT_ready[r], G + 5)
                    dve.tensor_copy(xs[:, u], bank[0]).then_inc(xs_ready[r], 1)

                def copy_y(G, k):
                    dve.wait_ge(ys_free[r], G + 1)
                    dve.wait_ge(y_ready[r], G + 1)
                    dve.tensor_copy(ys[:, k].rearrange("p a d -> p (a d)"), bank[5 + k % 2]).then_inc(ys_ready[r], 1)

                copy_x(0, 0)

                def turn(i, last):
                    for k in range(4):
                        G = i * 4 + k
                        if not (last and k == 3):
                            copy_x(G + 1, (k + 1) % 2)
                        copy_y(G, k)

                with dve.Fori(0, SGROUPS // 4 - 1) as i:
                    turn(i, False)
                turn(SGROUPS // 4 - 1, True)

                ch = new_chain()
                dve.sem_inc(x_done[r], 2)
                with dve.Fori(0, GROUPS // 2) as i:
                    with ch.turn(i, 8):
                        for u in range(2):
                            g = i * 2 + u
                            dve.wait_ge(yb_in[r][u], i * 16 + 16)
                            for j in range(GT):
                                t = g * GT + j
                                ch.did(dve.scalar_tensor_tensor(upd[:, u, j, :], yb[:, u, j, 0:D], wts[:, 0, tile(t)],
                                                                flat(x[:, tile(t), :]), ALU.mult, ALU.add))
                            ch.settle()
                            for j in range(GT):
                                t = g * GT + j
                                ins = dve.scalar_tensor_tensor(flat(x[:, tile(t), :]), yb[:, u, j, D:2 * D],
                                                               wts[:, 1, tile(t)], upd[:, u, j, :], ALU.mult, ALU.add)
                            ins.then_inc(x_done[r], 1)
                dve.wait_ge(x_done[r], GROUPS + 2)

            ffn(1)

            all_stats(2)

            def rotate(i, g, u):
                for m, (cos, sin) in enumerate((("cosq", "sinq"), ("cosk", "sink"))):
                    for c, tab in enumerate((cos, sin)):
                        dve.wait_ge(proj_ready, g * 4 + 2 * m + c + 1)
                        dve.tensor_tensor(rot[:, m, c], bank[2 + 2 * m + c], C[tab][:], ALU.mult).then_inc(rot_ready, 1)
                for m in range(2):
                    dve.wait_ge(rot_ready, g * 4 + 2 * m + 6)
                    dve.wait_ge(part3, g * 2 + m + 1)
                    dve.tensor_tensor(qk[:, m], rot[:, m, 0], rot[:, m, 1], ALU.add).then_inc(qk_ready, 1)

            dve.sem_inc(rot_ready, 4)
            norm(2, rotate)

            def softmax(g, s):
                par = s % 2
                hold(s_ready, g * STEPS + s + 1)
                sc = ps_s[par][:].rearrange("p (k w j) -> p k w j", w=2, j=P)
                dve.copy_predicated(sc[:, :, 0, :], causal[:].unsqueeze(1).broadcast_to([P, QUAD, P]), sc[:, :, 1, :])\
                    .then_inc(merged, 1)
                dve.wait_ge(merged, g * STEPS + s + 1)
                dve.tensor_reduce(nm[:, par], sc[:, :, 0, :], AX_X, ALU.max, negate=True).then_inc(nm_ready, 1)

            def take_out(g, j):
                dve.wait_ge(pv_done, (g * GT + j + 3) * NQUAD)
                dve.tensor_copy(oS[:, j % 2], bank[6 + j % 2]).then_inc(oS_ready, 1)

            def normalise(g, j):
                o = bank[6 + j % 2].rearrange("p (h c) -> p h c", c=VC)
                dve.wait_ge(oq_ready, g * GT + j + 1)
                dve.reciprocal(rden[:, j % 2].unsqueeze(2), o[:, :, HDB:VW]).then_inc(rden_ready, 1)
                dve.wait_ge(rden_ready, g * GT + j + 1)
                dve.tensor_tensor(ob[:, j % 2].rearrange("p (h c) -> p h c", c=HDB), o[:, :, 0:HDB],
                                  rden[:, j % 2].unsqueeze(2).broadcast_to([P, HB, HDB]), ALU.mult).then_inc(o_ready, 1)

            def add_out(g, j):
                t = g * GT + j
                dve.wait_ge(wo_done, t + 1)
                dve.tensor_tensor(flat(x[:, tile(t), :]), flat(x[:, tile(t), :]), bank[6 + j % 2][:, P:2 * P], ALU.add)\
                    .then_inc(x_added, 1)

            def slot(g, s):
                g0, s0, there = step_at(g, s, 0)
                if there:
                    softmax(g0, s0)
                for lag, do in ((TAKE_LAG, take_out), (NORM_LAG, normalise), (ADD_LAG, add_out)):
                    g0, s0, there = step_at(g, s, lag)
                    if there and s0 % NQUAD == 0:
                        do(g0, s0 // NQUAD)

            dve.wait_ge(bo_added, 1)
            slots(dve, slot)
            dve.wait_ge(x_added, TILES + 2)
            ffn(3)

        @block.tensor
        def _(pe):
            ident = C["ident"]
            pe.wait_ge(const_in, 16 * NCONST)
            pe.wait_ge(consts_made, 7)

            def transposed(r, g, u):
                pe.wait_ge(xn_ready[r], g + 1)
                for j in range(GT):
                    ins = pe.transpose(bank[u][:, j * P:(j + 1) * P], xn[:, u, j, :], ident[:])
                ins.then_inc(xT_ready[r], 1)
                pe.wait_ge(xnT_ready[r], g + 1)

            pe.sem_inc(xT_ready[0], 2)
            pe.sem_inc(fr_ready, 2)
            pe.matmul(bank[4][0:HAB, :], zeros[:, 0:HAB], zeros[:, :], start=True, stop=True)
            pe.sem_inc(sr_done, 2)
            with pe.Fori(0, GROUPS // 2) as i:
                for u in range(2):
                    g = i * 2 + u
                    transposed(0, g, u)
                    pe.matmul(bank[2 + u], W["WrT"][:], xnT[:, u], start=True, stop=True).then_inc(fr_ready, 1)
                    pe.wait_ge(attb_ready, g + 1)
                    pe.wait_ge(leaky_ready, g + 1)
                    pe.matmul(bank[4][0:HAB, :], attb[:, u], leaky[:, u], start=False, stop=True,
                              skip_group_check=True).then_inc(sr_done, 1)
            pe.wait_ge(a_dve, 2)
            for j in range(GT):
                ins = pe.transpose(bank[5][:, j * HAB:(j + 1) * HAB], pa[0:HAB, j * P:(j + 1) * P], ident[0:HAB, 0:HAB])
            ins.then_inc(a_pe, 1)
            pe.wait_ge(a_act, 2)
            pe.wait_ge(xn_saved[0], GROUPS + 2)
            for b in range(GROUPS):
                for j in range(GT):
                    ins = pe.matmul(bank[6][:, b * HA:(b + 1) * HA], h[:, b * GT + j, :],
                                    paT[:, j * HAB + b * HA:j * HAB + (b + 1) * HA], start=(j == 0), stop=(j == GT - 1))
            ins.then_inc(a_pe, 1)
            pe.wait_ge(a_act, 3)
            pe.matmul(bank[7][:, 0:HAB], W["WrT"][:], GT_sb[:], start=True, stop=True).then_inc(a_pe, 1)
            pe.wait_ge(a_dve, 3)
            for b in range(GROUPS):
                ins = pe.matmul(bank[b // GT][:, b % GT * D:(b % GT + 1) * D], ctxT[:, b:b + 1].broadcast_to([P, P]),
                                W["WfT"][:], start=True, stop=True)
                if b % GT == GT - 1:
                    ins.then_inc(a_pe, 1)

            def ffn(r):
                pe.sem_inc(xT_ready[r], 2)
                pe.sem_inc(lg_ready[r], 2)
                pe.sem_inc(lg_read[r], 2)
                with pe.Fori(0, GROUPS // 2) as i:
                    for u in range(2):
                        g = i * 2 + u
                        transposed(r, g, u)
                        pe.wait_ge(lg_read[r], g + 1)
                        for j in range(GT):
                            ins = pe.matmul(bank[2 + u][:, j * E:(j + 1) * E], xnT[:, u, j * P:(j + 1) * P], rwT[:],
                                            start=True, stop=True)
                        ins.then_inc(lg_ready[r], 1)
                pe.wait_ge(took_ready[r], 1)
                pe.matmul(bank[4][:, 0:TILES * E], before_bf[:], took[:], start=True, stop=True)
                pe.matmul(bank[5][:, 0:TILES * E], ones_bf[:], took[:], start=True, stop=True).then_inc(rank_ready[r], 1)
                pe.matmul(bank[6][:, 0:ST], zeros[:, 0:P], zeros[:, 0:ST], start=True, stop=True)
                pe.sem_inc(hot_used[r], 2)
                with pe.Fori(0, TILES // 2) as i:
                    for u in range(2):
                        pe.wait_ge(hot_ready[r], i * 2 + u + 1)
                        for c in range(TOPK):
                            ins = pe.matmul(bank[6][:, 0:ST], hot_lo[:, u, c], hot_hi[:, u, c], start=False, stop=True,
                                            skip_group_check=True)
                        ins.then_inc(hot_used[r], 1)

                def turn_tokens(i, k):
                    pe.wait_ge(g_in[r][k], i * (16 * SGT) + 16 * SGT)
                    for j in range(SGT):
                        ins = pe.transpose(bank[0][:, j * P:(j + 1) * P], xg[:, k, j, :], ident[:])
                    ins.then_inc(xgT_ready[r], 1)

                pe.sem_inc(xgT_ready[r], 4)
                turn_tokens(0, 0)

                def turn(i, last):
                    for k in range(4):
                        G, u = i * 4 + k, k // 2
                        if k % 2 == 0:
                            pe.wait_ge(w_in[r][u], i * 32 + 32)
                        pe.wait_ge(xs_ready[r], G + 1)
                        for c in range(FC):
                            pe.matmul(bank[1 + c], w1b[:, u, c * P:(c + 1) * P], xs[:, k % 2], start=True, stop=True)\
                                .then_inc(h_ready[r], 1)
                        if not (last and k == 3):
                            turn_tokens(i + (k + 1) // 4, (k + 1) % 4)
                        for j in range(SGT):
                            for c in range(FC):
                                if j == 0:
                                    pe.wait_ge(gelu_done[r], G * FC + (c + 1))
                                ins = pe.matmul(bank[5 + k % 2][:, j * D:(j + 1) * D], hid[:, c, j * P:(j + 1) * P],
                                                w2b[:, u, c, :], start=(c == 0), stop=(c == FC - 1))
                        ins.then_inc(y_ready[r], 1)

                with pe.Fori(0, SGROUPS // 4 - 1) as i:
                    turn(i, False)
                turn(SGROUPS // 4 - 1, True)

            ffn(1)

            pe.sem_inc(xT_ready[2], 2)
            pe.sem_inc(v_ready, 2)
            with pe.Fori(0, GROUPS // 2) as i:
                for u in range(2):
                    g = i * 2 + u
                    transposed(2, g, u)
                    for m, k in enumerate(("WqT", "WqrT", "WkT", "WkrT")):
                        pe.wait_ge(rot_ready, g * 4 + m + 1)
                        pe.matmul(bank[2 + m], W[k][:], xnT[:, u], start=True, stop=True).then_inc(proj_ready, 1)
                    for j in range(GT):
                        ins = pe.matmul(bank[6 + u][:, j * D:(j + 1) * D], xnT[:, u, j * P:(j + 1) * P], W["WvT"][:],
                                        start=True, stop=True)
                    ins.then_inc(v_ready, 1)

            def scores(g, s):
                j, q = divmod(s, NQUAD)
                if q == 0:
                    pe.wait_ge(qk_in[j], g * (16 * 2 * PARTS) + 16 * 2 * PARTS)
                if not isinstance(g, int) or g * STEPS + s >= 2:
                    pe.wait_ge(p_ready, g * STEPS + (s - 1))
                for k in range(QUAD):
                    hc = slice((q * QUAD + k) * P, (q * QUAD + k + 1) * P)
                    ins = pe.matmul(ps_s[s % 2][:, 2 * k * P:(2 * k + 2) * P].rearrange("p (w j) -> p w j", j=P),
                                    qb[0:KR1, j, hc], kb[0:KR1, j:j + 2, hc], start=True, stop=True)
                ins.then_inc(s_ready, 1)

            def turn_weights(g, s):
                if not isinstance(g, int) or g * STEPS + s >= 2:
                    pe.wait_ge(pT_copied, g * STEPS + (s - 1))
                pe.wait_ge(p_ready, g * STEPS + s + 1)
                for k in range(QUAD):
                    ins = pe.transpose(bank[4 + s % 2][:, k * P:(k + 1) * P], pb[:, s % LANES, k, :], ident[:])
                ins.then_inc(pT_ready, 1)

            def weigh(g, s):
                j, q = divmod(s, NQUAD)
                if q == 0:
                    pe.wait_ge(vt_ready, (g * GT + j) * 2 + 2)
                    pe.wait_ge(x_added, g * GT + j + 1)
                pe.wait_ge(pTc_ready, g * STEPS + s + 1)
                for share, v in ((pT, vp), (pTc, vd)):
                    for k in range(QUAD):
                        ins = pe.matmul(bank[6 + j % 2][k * VC:(k + 1) * VC, q * P:(q + 1) * P],
                                        v[:, j % 2, q * QUAD + k, :], share[:, s % LANES, k * P:(k + 1) * P],
                                        start=share is pT, stop=share is pTc, tile_position=(0, k * VC))
                ins.then_inc(pv_done, 1)

            def turn_results(g, j):
                pe.wait_ge(oS_ready, g * GT + j + 1)
                for q in range(NQUAD):
                    ins = pe.transpose(bank[6 + j % 2][:, q * P:(q + 1) * P], oS[:, j % 2, q * P:(q + 1) * P], ident[:])
                ins.then_inc(oq_ready, 1)

            def turn_out(g, j):
                pe.wait_ge(o_ready, g * GT + j + 1)
                pe.transpose(bank[6 + j % 2][:, 0:P], ob[:, j % 2], ident[:]).then_inc(oT_ready, 1)

            def project(g, j):
                pe.wait_ge(oT_copied, g * GT + j + 1)
                pe.matmul(bank[6 + j % 2][:, P:2 * P], oT[:, j % 2], W["WoT"][:], start=True, stop=True).then_inc(wo_done, 1)

            pe.sem_inc(pv_done, 2 * NQUAD)
            pe.sem_inc(x_added, 2)
            pe.wait_ge(v_copied, GROUPS)
            pe.wait_ge(rot_ready, 4 * GROUPS + 4)

            def slot(g, s):
                for lag, do in ((0, scores), (TURN_LAG, turn_weights), (WEIGH_LAG, weigh)):
                    g0, s0, there = step_at(g, s, lag)
                    if there:
                        do(g0, s0)
                for lag, do in ((TURN_RES_LAG, turn_results), (OT_LAG, turn_out), (PROJ_LAG, project)):
                    g0, s0, there = step_at(g, s, lag)
                    if there and s0 % NQUAD == 0:
                        do(g0, s0 // NQUAD)

            slots(pe, slot)
            ffn(3)


def kernel(**inputs):
    import concourse.bacc as bacc
    from concourse.bass_utils import run_bass_kernel_spmd

    nc = bacc.Bacc("TRN2", target_bir_lowering=False, num_devices=1)
    i = {k: np.ascontiguousarray(v) for k, v in inputs.items()}
    rows = np.arange(D).reshape(HB, HDB)
    swap = rows.reshape(HB, 2, HDB // 2)[:, ::-1].reshape(HB, HDB).T.reshape(-1)
    rows = rows.T.reshape(-1)
    arrays = {
        "x": i["L0_attn_a_h"].reshape(B * N, D),
        "WrT": i["L0_attn_a_Wr"].T, "WfT": i["L0_attn_a_Wf"].T,
        "WqT": i["L0_attn_b_Wq"][rows].T, "WqrT": i["L0_attn_b_Wq"][swap].T,
        "WkT": i["L0_attn_b_Wk"][rows].T, "WkrT": i["L0_attn_b_Wk"][swap].T,
        "WvT": i["L0_attn_b_Wv"].T, "WoT": i["L0_attn_b_Wo"].T,
        "rwT": i["L0_ffn_router_w"].T,
        "attr": np.tile(i["L0_attn_a_att_r"].reshape(HDA), HA).reshape(D, 1),
        "gamma": i["L0_attn_a_ln_gamma"].reshape(1, D), "beta": i["L0_attn_a_ln_beta"].reshape(1, D),
        "bo": i["L0_attn_b_bo"].reshape(1, D),
        "w1": i["L0_ffn_w1"], "w2": i["L0_ffn_w2"],
    }
    arrays.update({"c_" + k: v for k, v in tables().items()})
    arrays = {"in_" + k: np.ascontiguousarray(v) for k, v in arrays.items()}
    aps = {k[3:]: nc.dram_tensor(k, v.shape, mybir.dt.from_np(v.dtype), kind="ExternalInput").ap()
           for k, v in arrays.items()}
    out = nc.dram_tensor("out_dram", (B * N, D), F32, kind="ExternalOutput").ap()
    hybrid_block(nc, aps, out)
    r = run_bass_kernel_spmd(nc, [arrays], core_ids=[0])
    return r.results[0]["out_dram"].reshape(B, N, D)
```

```python
from contextlib import ExitStack, contextmanager

import numpy as np

import concourse.bass as bass
from concourse import mybir

P = 128
D = 128
B, N = 8, 512
TILES = B * N // P
GT = N // P
GROUPS = TILES // GT
HA = 8
HDA = D // HA
HB = 16
HDB = D // HB
E = 8
FF = 512
FC = FF // P
TOPK = 2
SLOTS = B * N * TOPK
SGT = 4
SG = SGT * P
SGROUPS = SLOTS // SG
ST = SLOTS // P
EPS = 1e-5
PARTS = 3
KROWS = PARTS * PARTS * HDB
KR1 = KROWS + 1
QUAD = 4
NQUAD = HB // QUAD
STEPS = GT * NQUAD
VW = HDB + 1
VC = 32
LANES = 4
NEG = -1.0e30

F32 = mybir.dt.float32
BF16 = mybir.dt.bfloat16
I32 = mybir.dt.int32
ALU = mybir.AluOpType
ACT = mybir.ActivationFunctionType
AX_X = mybir.AxisListType.X


class Chain:

    def __init__(self, eng, sem):
        self.eng, self.sem, self.base, self.n = eng, sem, 0, 0

    def did(self, ins):
        ins.then_inc(self.sem, 1)
        self.n += 1

    def settle(self):
        self.eng.wait_ge(self.sem, self.base + self.n)

    @contextmanager
    def turn(self, i, per):
        start, self.base = self.n, i * per
        yield
        assert self.n - start == per, (self.n - start, per)
        self.n = start

    def after(self, turns, per):
        self.base, self.n = 0, self.n + turns * per


def step_at(g, s, lag):
    q, r = divmod(s - lag, STEPS)
    return g + q, r, not isinstance(g, int) or 0 <= g + q < GROUPS


def tables():
    p, t, k = np.arange(P), np.arange(TILES), np.arange(TOPK)
    f = np.float32
    c = {}
    c["ident"] = np.eye(P, dtype=f)
    c["before"] = (p[:, None] < p[None, :]).astype(f)
    c["iota"] = np.tile(np.arange(P, dtype=f), (P, 1))
    c["entry_p"] = (TOPK * p[:, None] + k[None, :]).astype(f)
    c["entry_t"] = np.tile(t.astype(f), (P, 1))
    c["order"] = np.tile((E - np.arange(E)).astype(f), (P, 1))
    c["head_of"] = (p[:, None] // HDA == np.arange(HA)[None, :]).astype(f)
    c["causal"] = (p[None, :] <= p[:, None]).astype(np.int32)
    c["causal_t"] = (p[:, None] <= p[None, :]).astype(f)
    inv = (f(1.0) / np.power(f(10000.0), np.arange(0, HDB, 2, dtype=f) / f(HDB))).astype(f)
    ang = np.arange(N, dtype=f)[:, None] * inv[None, :]
    ang = np.concatenate([ang, ang], -1).T.astype(f)
    sign = np.where(np.arange(HDB) < HDB // 2, -1.0, 1.0)[:, None]
    cos, sin = np.cos(ang.astype(np.float64)), np.sin(ang.astype(np.float64)) * sign
    for name, s in (("q", HDB ** -0.5), ("k", 1.0)):
        c["cos" + name] = np.repeat(cos * s, HB, 0).astype(f)
        c["sin" + name] = np.repeat(sin * s, HB, 0).astype(f)
    c["mark"] = np.full((1, HB * P), NEG, dtype=f)
    return c


def hybrid_block(nc, a, out):
    with ExitStack() as ctx:
        def sb(name, shape, dt=F32):
            return ctx.enter_context(nc.sbuf_tensor("sb_" + name, shape, dt))

        def sem(name):
            return ctx.enter_context(nc.semaphore(name))

        def sems(name, n):
            return [sem(f"{name}{k}") for k in range(n)]

        def psum(name, cols):
            return ctx.enter_context(nc.psum_tensor(name, [P, cols], F32))

        ps_s = [psum("ps_s0", 1024), psum("ps_s1", 1024)]
        bank = [ps_s[0][:, 0:512], ps_s[0][:, 512:1024], ps_s[1][:, 0:512], ps_s[1][:, 512:1024]]
        bank += [psum(f"bank{k}", 512)[:, :] for k in range(4, 8)]

        c_shapes = {"ident": P, "before": P, "iota": P, "entry_p": TOPK, "entry_t": TILES, "order": E, "head_of": HA,
                    "causal_t": P, "cosq": N, "sinq": N, "cosk": N, "sink": N}
        C = {k: sb("c_" + k, [P, w]) for k, w in c_shapes.items()}
        causal = sb("causal", [P, P], I32)
        W = {k: sb(k, [P, D]) for k in ("WrT", "WfT", "WqT", "WqrT", "WkT", "WkrT", "WvT", "WoT")}
        rwT = sb("rwT", [P, P])
        attr = sb("attr", [P, 1])
        gamma = sb("gamma", [P, D])
        beta = sb("beta", [P, D])
        bo = sb("bo", [P, D])
        zeros = sb("zeros", [P, 512])
        ones_bf = sb("ones_bf", [P, P], BF16)
        before_bf = sb("before_bf", [P, P], BF16)

        x = sb("x", [P, TILES, D])
        mean = sb("mean", [P, TILES])
        vareps = sb("vareps", [P, TILES])
        rstd = sb("rstd", [P, TILES])
        root = sb("root", [P, TILES])
        seed = sb("seed", [P, TILES], I32)
        stat6 = sb("stat6", [P, 2 * GT, 6])
        mv = sb("mv", [P, 2 * GT, 2])
        xn = sb("xn", [P, 2, GT, D])
        xnT = sb("xnT", [P, 2, GT * P])
        upd = sb("upd", [P, 2, GT, D])

        h = sb("h", [P, TILES, D])
        leaky = sb("leaky", [P, 2, N])
        attpad = sb("attpad", [P, 2 * GROUPS * HA])
        attb = sb("attb", [P, 2, GROUPS * HA])
        HAB = GROUPS * HA
        nmax = sb("nmax", [P, 1])
        psum_row = sb("psum_row", [P, 1])
        prec = sb("prec", [P, 1])
        pa = sb("pa", [P, N])
        paT = sb("paT", [P, GT * HAB])
        GT_sb = sb("GT_sb", [P, HAB])
        ctxm = sb("ctxm", [P, HAB])
        ctxT = sb("ctxT", [P, GROUPS])
        fh = sb("fh", [P, GROUPS, D])

        lg = sb("lg", [P, TILES, E])
        top = sb("top", [P, TOPK, TILES])
        pick = sb("pick", [P, TILES, E])
        best = sb("best", [P, TILES])
        hot = sb("hot", [P, TOPK, TILES, E])
        wts = sb("wts", [P, TOPK, TILES])
        den = sb("den", [P, TILES])
        took = sb("took", [P, TILES * E], BF16)
        tot = sb("tot", [P, E, TILES])
        onesf = sb("onesf", [P, E * TILES])
        incl = sb("incl", [P, E, TILES])
        posf = sb("posf", [P, TILES, E])
        pos = sb("pos", [P, TOPK, TILES])
        pos_i = sb("pos_i", [P, 2, TOPK * TILES], I32)
        pos_hl = sb("pos_hl", [P, 2, TOPK * TILES])
        hot_lo = sb("hot_lo", [P, 2, TOPK, GT, P], BF16)
        hot_hi = sb("hot_hi", [P, 2, TOPK, GT, ST], BF16)
        hot_en = sb("hot_en", [P, 2, TOPK, GT, 2, ST], BF16)
        entry_pt = sb("entry_pt", [P, 2 * ST])
        entry_i = sb("entry_i", [P, ST], I32)
        token_i = sb("token_i", [P, ST], I32)

        w1b = sb("w1b", [P, 2, FF])
        w2b = sb("w2b", [P, 2, FC, D])
        tcol = sb("tcol", [P, 4, SGT], I32)
        ecol = sb("ecol", [P, 4, SGT], I32)
        xg = sb("xg", [P, 4, SGT, D])
        xs = sb("xs", [P, 2, SG])
        hid = sb("hid", [P, FC, SG])
        ys = sb("ys", [P, 4, SGT, D])
        yb = sb("yb", [P, 2, GT, TOPK * D])

        rot = hid[:].rearrange("p (m c) n -> p m c n", m=2)
        qk = yb[:].rearrange("p u t c -> p u (t c)").rearrange("p u (m n) -> p u m n", n=N)
        part = [v[:].rearrange("p a b c -> p (a b c)").bitcast(BF16)[:, 0:2 * PARTS * N]
                .rearrange("p (m c n) -> p m c n", m=2, c=PARTS) for v in (xg, ys)]
        vE = sb("vE", [P, TILES + 1, HB * VW])
        qb = h[:].rearrange("p t d -> p (t d)").bitcast(BF16).rearrange("p (j c) -> p j c", j=GT)
        kb = sb("kb", [P, GT + 1, HB * P], BF16)
        nm = sb("nm", [P, 2, QUAD])
        pb = yb[:].rearrange("p u t c -> p (u t c)").rearrange("p (b k j) -> p b k j", b=LANES, j=P)
        pT = xg[:].rearrange("p u k q -> p u (k q)")
        pTc = ys[:].rearrange("p u k q -> p u (k q)")
        vp = sb("vp", [P, 2, HB, VC])
        vd = sb("vd", [P, 2, HB, VC])
        oS = sb("oS", [P, 2, NQUAD * P])
        rden = sb("rden", [P, 2, HB])
        ob = sb("ob", [P, 2, D])
        oT = sb("oT", [P, 2, P])
        markf = sb("markf", [P, 1])

        def dram(name, shape, dt=F32):
            return nc.dram_tensor(name, shape, dt).ap()

        xn_dram = [dram(f"xn_dram{r}", (B * N, D)) for r in range(2)]
        y_dram = [dram(f"y_dram{r}", (SLOTS, D)) for r in range(2)]
        q_dram = dram("q_dram", (PARTS, TILES, HDB, HB, P), BF16)
        k_dram = dram("k_dram", (PARTS, TILES, HDB, HB, P), BF16)

        const_in = sem("const_in")
        x_in = sems("x_in", 2)
        consts_made = sem("consts_made")
        pool_chain = sem("pool_chain")
        act_chain = sem("act_chain")
        dve_chain = [sem(f"dve_chain{k}") for k in range(12)]
        spacer = {e: sem("spacer_" + e) for e in ("pool", "act", "dve")}
        xn_ready = sems("xn_ready", 4)
        h_kept = sem("h_kept")
        xn_out = {r: sems(f"xn_out{r}_", 2) for r in (1, 3)}
        xT_ready = sems("xT_ready", 4)
        xnT_ready = sems("xnT_ready", 4)

        fr_ready = sem("fr_ready")
        fr_scaled = sem("fr_scaled")
        fills = sem("fills")
        leaky_ready = sem("leaky_ready")
        sr_done = sem("sr_done")
        attb_ready = sem("attb_ready")
        a_pe = sem("a_pe")
        a_act = sem("a_act")
        a_dve = sem("a_dve")
        beta_added = sem("beta_added")

        lg_ready = {r: sem(f"lg_ready{r}") for r in (1, 3)}
        lg_read = {r: sem(f"lg_read{r}") for r in (1, 3)}
        took_ready = {r: sem(f"took_ready{r}") for r in (1, 3)}
        rank_ready = {r: sem(f"rank_ready{r}") for r in (1, 3)}
        hi_ready = {r: sem(f"hi_ready{r}") for r in (1, 3)}
        en_ready = {r: sem(f"en_ready{r}") for r in (1, 3)}
        ent_ready = {r: sem(f"ent_ready{r}") for r in (1, 3)}
        hot_ready = {r: sem(f"hot_ready{r}") for r in (1, 3)}
        hot_used = {r: sem(f"hot_used{r}") for r in (1, 3)}
        wd_ready = {r: sem(f"wd_ready{r}") for r in (1, 3)}
        we_ready = {r: sem(f"we_ready{r}") for r in (1, 3)}
        index_ready = {r: sem(f"index_ready{r}") for r in (1, 3)}
        w_in = {r: sems(f"w_in{r}_", 2) for r in (1, 3)}
        g_in = {r: sems(f"g_in{r}_", 4) for r in (1, 3)}
        xgT_ready = {r: sem(f"xgT_ready{r}") for r in (1, 3)}
        xs_ready = {r: sem(f"xs_ready{r}") for r in (1, 3)}
        h_ready = {r: sem(f"h_ready{r}") for r in (1, 3)}
        gelu_done = {r: sem(f"gelu_done{r}") for r in (1, 3)}
        y_ready = {r: sem(f"y_ready{r}") for r in (1, 3)}
        ys_ready = {r: sem(f"ys_ready{r}") for r in (1, 3)}
        ys_free = {r: sem(f"ys_free{r}") for r in (1, 3)}
        y_out = {r: sems(f"y_out{r}_", 4) for r in (1, 3)}
        yb_in = {r: sems(f"yb_in{r}_", 2) for r in (1, 3)}
        x_done = {r: sem(f"x_done{r}") for r in (1, 3)}

        proj_ready = sem("proj_ready")
        rot_ready = sem("rot_ready")
        qk_ready = sem("qk_ready")
        part1 = sem("part1")
        rest1 = sem("rest1")
        part2 = sem("part2")
        part3 = sem("part3")
        parts_out = sems("parts_out", 2)
        parts_free = sem("parts_free")
        v_ready = sem("v_ready")
        v_copied = sem("v_copied")
        bo_added = sem("bo_added")
        mark_in = sem("mark_in")
        mark_made = sem("mark_made")
        mark_ready = sem("mark_ready")
        qk_in = sems("qk_in", GT)
        s_ready = sem("s_ready")
        merged = sem("merged")
        rden_ready = sem("rden_ready")
        nm_ready = sem("nm_ready")
        p_ready = sem("p_ready")
        pT_ready = sem("pT_ready")
        pT_copied = sem("pT_copied")
        pTc_ready = sem("pTc_ready")
        vt_ready = sem("vt_ready")
        pv_done = sem("pv_done")
        oS_ready = sem("oS_ready")
        oq_ready = sem("oq_ready")
        o_ready = sem("o_ready")
        x_added = sem("x_added")
        oT_ready = sem("oT_ready")
        oT_copied = sem("oT_copied")
        wo_done = sem("wo_done")
        out_done = sem("out_done")

        xnT_read = {0: fr_ready, 1: lg_ready[1], 2: v_ready, 3: lg_ready[3]}

        block = ctx.enter_context(nc.Block())
        NCONST = len(C) + 1 + len(W) + 5

        def by_group(eng, body, tail):
            for g in range(2):
                body(g, g)
            with eng.Fori(1, GROUPS // 2) as i:
                for u in range(2):
                    body(i * 2 + u, u)
            for g in range(GROUPS, GROUPS + tail):
                body(g, g % 2)

        def have(g, lag):
            return not isinstance(g, int) or 0 <= g - lag < GROUPS

        def later(g):
            return not isinstance(g, int) or g >= 2

        def tile(t):
            return bass.ds(t, 1)

        TURN_LAG, WEIGH_LAG = 2, 5
        TAKE_LAG, TURN_RES_LAG, NORM_LAG, TURN_OUT_LAG, OT_LAG, PROJ_LAG, ADD_LAG = 9, 9, 10, 10, 11, 11, 12

        def slots(eng, slot):
            for s in range(STEPS):
                slot(0, s)
            with eng.Fori(1, GROUPS) as g:
                for s in range(STEPS):
                    slot(g, s)
            for s in range(ADD_LAG + 1):
                slot(GROUPS, s)

        def flat(ap):
            return ap.rearrange("p a d -> p (a d)")

        @block.sync
        def _(sp):
            xt = a["x"].rearrange("(t p) d -> p t d", p=P)
            for half in range(2):
                s = slice(half * TILES // 2, (half + 1) * TILES // 2)
                sp.dma_start(x[:, s, :], xt[:, s, :]).then_inc(x_in[half], 16)
            for k in C:
                sp.dma_start(C[k][:], a["c_" + k]).then_inc(const_in, 16)
            sp.dma_start(causal[:], a["c_causal"]).then_inc(const_in, 16)
            for k in W:
                sp.dma_start(W[k][:], a[k]).then_inc(const_in, 16)
            sp.dma_start(rwT[:, 0:E], a["rwT"]).then_inc(const_in, 16)
            sp.dma_start(attr[:], a["attr"]).then_inc(const_in, 16)
            for dst, k in ((gamma, "gamma"), (beta, "beta"), (bo, "bo")):
                sp.dma_start(dst[:], a[k].broadcast_to([P, D])).then_inc(const_in, 16)

            def ffn(r):
                n = r // 2
                rows = xn_dram[n].rearrange("(t p) d -> p t d", p=P)
                with sp.Fori(0, GROUPS // 2) as i:
                    for u in range(2):
                        g = i * 2 + u
                        sp.wait_ge(xn_ready[r], g + 1)
                        sp.dma_start(rows[:, bass.ds(g * GT, GT), :], xn[:, u]).then_inc(xn_out[r][u], 16)
                sp.sem_inc(ys_free[r], 4)
                w1r = a["w1"].rearrange("e d f -> d e f")
                w2r = a["w2"].rearrange("e (c f) d -> f e c d", f=P)

                def load_expert(e, u):
                    sp.dma_start(w1b[:, u], flat(w1r[:, tile(e), :])).then_inc(w_in[r][u], 16)
                    sp.dma_start(w2b[:, u], w2r[:, tile(e)].rearrange("f e c d -> f (e c) d")).then_inc(w_in[r][u], 16)

                for u in range(2):
                    load_expert(u, u)
                with sp.Fori(0, SGROUPS // 4) as i:
                    for k in range(4):
                        sp.wait_ge(y_out[r][k], i * (16 * SGT) + 16 * SGT)
                        sp.sem_inc(ys_free[r], 1)
                        if k % 2 == 1:
                            sp.wait_ge(y_ready[r], i * 4 + k + 1)
                            load_expert((i * 2 + 2 + k // 2) % E, k // 2)
                for u in range(2):
                    sp.wait_ge(w_in[r][u], 32 * (E // 2 + 1))
                yr = y_dram[n].rearrange("(t p k) d -> p t (k d)", p=P, k=TOPK)
                with sp.Fori(0, GROUPS // 2) as i:
                    for u in range(2):
                        g = i * 2 + u
                        sp.wait_ge(x_done[r], g + 1)
                        sp.dma_start(yb[:, u], yr[:, bass.ds(g * GT, GT), :]).then_inc(yb_in[r][u], 16)

            ffn(1)

            sp.sem_inc(parts_free, 2)
            src = (q_dram, k_dram)
            GROUP_OUT = 16 * 2 * PARTS

            def store_parts(i, u):
                sp.wait_ge(part3, i * 4 + (2 * u + 6))
                for m in range(2):
                    for c in range(PARTS):
                        dst = src[m][c].rearrange("t d h n -> (d h) t n")[:, bass.ds((i * 2 + u) * GT, GT), :]
                        sp.dma_start(dst, part[u][:, m, c, :].rearrange("p (t n) -> p t n", n=P))\
                            .then_inc(parts_out[u], 16)

            def stored(i, u):
                sp.wait_ge(parts_out[u], i * GROUP_OUT + GROUP_OUT)
                sp.sem_inc(parts_free, 1)

            with sp.Fori(0, GROUPS // 2) as i:
                for u in range(2):
                    store_parts(i, u)
                    stored(i, u)

            def load_qk(g, j):
                t = g * GT + j
                for c in range(PARTS):
                    rows = slice(c * PARTS * HDB, (c + 1) * PARTS * HDB)
                    qsrc = q_dram[:, tile(t)].rearrange("a t d h n -> a (t d) (h n)")
                    ksrc = k_dram[c:c + 1, tile(t)].rearrange("c t d h n -> c (t d) (h n)")
                    sp.dma_start(qb[rows, j], qsrc).then_inc(qk_in[j], 16)
                    sp.dma_start(kb[rows, j + 1], ksrc.broadcast_to([PARTS, HDB, HB * P])).then_inc(qk_in[j], 16)

            sp.wait_ge(mark_ready, 1)
            for j in range(GT):
                load_qk(0, j)
            with sp.Fori(1, GROUPS) as g:
                for j in range(GT):
                    sp.wait_ge(s_ready, (g - 1) * (2 * STEPS) + 2 * min(j + 2, GT) * NQUAD)
                    load_qk(g, j)

            ffn(3)
            ot = out.rearrange("(t p) d -> p t d", p=P)
            with sp.Fori(0, GROUPS) as g:
                sp.wait_ge(x_done[3], g + 3)
                sp.dma_start(ot[:, bass.ds(g * GT, GT), :], x[:, bass.ds(g * GT, GT), :]).then_inc(out_done, 16)
            sp.wait_ge(out_done, 16 * GROUPS)

        @block.gpsimd
        def _(pool):
            ch = Chain(pool, pool_chain)

            def hold(s, value):
                pool.wait_ge(s, value)
                pool.sem_inc(spacer["pool"], 1)

            pool.memset(rwT[:, E:P], 0.0).then_inc(consts_made, 1)
            pool.memset(zeros[:], 0.0).then_inc(consts_made, 1)
            pool.memset(ones_bf[:], 1.0).then_inc(consts_made, 1)
            pool.memset(onesf[:], 1.0).then_inc(consts_made, 1)
            pool.memset(attpad[:], 0.0).then_inc(consts_made, 1)

            pool.wait_ge(consts_made, 7)
            pool.wait_ge(const_in, 16 * NCONST)
            with pool.Fori(0, GROUPS // 2) as i:
                for u in range(2):
                    g = i * 2 + u
                    hold(xn_ready[0], g + 1)
                    pool.tensor_copy(h[:, bass.ds(g * GT, GT), :], xn[:, u]).then_inc(h_kept, 1)
                    hold(sr_done, g + 1)
                    pool.tensor_copy(attb[:, u], attpad[:, bass.ds(GROUPS * HA - HA - g * HA, GROUPS * HA)])\
                        .then_inc(attb_ready, 1)
            pool.tensor_tensor(x[:], x[:], beta[:].unsqueeze(1).broadcast_to([P, TILES, D]), ALU.add)\
                .then_inc(beta_added, 1)

            def ffn(r):
                n = r // 2
                if r == 1:
                    pool.wait_ge(xn_ready[1], 1)
                    pool.memset(vE[:], 1.0).then_inc(fills, 1)
                    pool.memset(qb, 1.0).then_inc(fills, 1)
                    pool.memset(kb[:], 0.0).then_inc(fills, 1)
                    pool.memset(vp[:], 0.0).then_inc(fills, 1)
                    pool.memset(vd[:], 0.0).then_inc(fills, 1)
                with pool.Fori(0, GROUPS // 2) as i:
                    for u in range(2):
                        g = i * 2 + u
                        hold(hot_used[r], g + 1)
                        hold(hi_ready[r], g + 1)
                        pool.tensor_tensor(
                            hot_en[:, u, :, :, 1, :], hot_hi[:, u],
                            C["entry_t"][:, bass.ds(g * GT, GT)].unsqueeze(1).unsqueeze(3)
                            .broadcast_to([P, TOPK, GT, ST]), ALU.mult).then_inc(ent_ready[r], 1)
                pool.wait_ge(index_ready[r], 1)

                def columns(G, k):
                    ch.did(pool.tensor_copy(tcol[:, k], token_i[:, bass.ds(G * SGT, SGT)]))
                    ch.did(pool.tensor_copy(ecol[:, k], entry_i[:, bass.ds(G * SGT, SGT)]))

                def gather(k):
                    for j in range(SGT):
                        pool.indirect_dma_start(xg[:, k, j, :], None, xn_dram[n],
                                                bass.IndirectOffsetOnAxis(ap=tcol[:, k, j:j + 1], axis=0))\
                            .then_inc(g_in[r][k], 16)

                def scatter(k):
                    for j in range(SGT):
                        pool.indirect_dma_start(y_dram[n], bass.IndirectOffsetOnAxis(ap=ecol[:, k, j:j + 1], axis=0),
                                                ys[:, k, j, :], None).then_inc(y_out[r][k], 16)

                def settle_hold():
                    ch.settle()
                    pool.sem_inc(spacer["pool"], 1)

                for u in range(2):
                    pool.wait_ge(xn_out[r][u], 16 * (GROUPS // 2))
                for k in range(2):
                    columns(k, k)
                ch.settle()
                for k in range(2):
                    gather(k)

                def turn(i, last):
                    for k in range(4):
                        G = i * 4 + k
                        if not (last and k >= 2):
                            k2 = (k + 2) % 4
                            hold(xgT_ready[r], G + 3)
                            hold(ys_free[r], G + 3)
                            columns(G + 2, k2)
                            settle_hold()
                            gather(k2)
                        hold(ys_ready[r], G + 1)
                        scatter(k)

                turns = SGROUPS // 4
                with pool.Fori(0, turns - 1) as i:
                    with ch.turn(i, 8):
                        turn(i, False)
                ch.after(turns - 1, 8)
                turn(turns - 1, True)
                for k in range(4):
                    pool.wait_ge(y_out[r][k], 16 * SGT * turns)
            ffn(1)

            pool.sem_inc(part3, 4)

            def rests(g, u):
                if have(g, 1):
                    for m in range(2):
                        pool.wait_ge(part2, g * 2 + m - 1)
                        pool.tensor_tensor(part[1 - u][:, m, 2], qk[:, 1 - u, m], part[1 - u][:, m, 1], ALU.subtract)\
                            .then_inc(part3, 1)
                if have(g, 0):
                    for m in range(2):
                        pool.wait_ge(part1, g * 2 + m + 1)
                        pool.tensor_tensor(qk[:, u, m], qk[:, u, m], part[u][:, m, 0], ALU.subtract).then_inc(rest1, 1)

            by_group(pool, rests, 1)
            pool.wait_ge(xn_ready[2], GROUPS)
            pool.tensor_tensor(x[:], x[:], bo[:].unsqueeze(1).broadcast_to([P, TILES, D]), ALU.add)\
                .then_inc(bo_added, 1)
            pool.wait_ge(v_copied, GROUPS + 2)
            def heads(v):
                return v.rearrange("p t (h c) -> p (t h) c", c=VW)

            def values(g, j):
                t = g * GT + j
                hold(pv_done, (t + 1) * NQUAD)
                pool.tensor_copy(vp[:, j % 2, :, 0:VW], heads(vE[:, tile(t), :])).then_inc(vt_ready, 1)
                pool.tensor_tensor(vd[:, j % 2, :, 0:VW], heads(vE[:, tile(t + 1), :]), heads(vE[:, tile(t), :]),
                                   ALU.subtract).then_inc(vt_ready, 1)

            with pool.Fori(0, GROUPS) as g:
                for s in range(STEPS):
                    if s % NQUAD == 0:
                        values(g, s // NQUAD)
                    pool.wait_ge(pT_copied, g * STEPS + s + 1)
                    pool.tensor_tensor(pTc[:, s % LANES].rearrange("p (k q) -> p k q", q=P),
                                       pT[:, s % LANES].rearrange("p (k q) -> p k q", q=P),
                                       C["causal_t"][:].unsqueeze(1).broadcast_to([P, QUAD, P]), ALU.mult)\
                        .then_inc(pTc_ready, 1)

            ffn(3)

        @block.scalar
        def _(act):
            ch = Chain(act, act_chain)

            def hold(s, value):
                act.wait_ge(s, value)
                act.sem_inc(spacer["act"], 1)

            def copy_xT(r, g, u):
                act.wait_ge(xnT_read[r], g + 1)
                act.wait_ge(xT_ready[r], g + 3)
                act.activation(xnT[:, u], bank[u], ACT.Copy).then_inc(xnT_ready[r], 1)

            with act.Fori(0, GROUPS // 2) as i:
                for u in range(2):
                    copy_xT(0, i * 2 + u, u)
            act.wait_ge(a_dve, 1)
            act.activation(pa[0:HAB, :], bank[4][0:HAB, :], ACT.Exp, bias=nmax[0:HAB, :],
                           accum_out=psum_row[0:HAB, :]).then_inc(a_act, 1)
            act.wait_ge(a_pe, 1)
            act.activation(paT[:], bank[5][:, 0:GT * HAB], ACT.Copy).then_inc(a_act, 1)
            act.wait_ge(a_pe, 2)
            act.activation(GT_sb[:], bank[6][:, 0:HAB], ACT.Copy).then_inc(a_act, 1)
            for b in range(2):
                act.wait_ge(a_pe, 4 + b)
                act.activation(fh[:, b * GT:(b + 1) * GT, :].rearrange("p a d -> p (a d)"), bank[b], ACT.Copy)\
                    .then_inc(a_act, 1)

            def ffn(r):
                with act.Fori(0, GROUPS // 2) as i:
                    for u in range(2):
                        copy_xT(r, i * 2 + u, u)
                act.wait_ge(wd_ready[r], 1)
                act.activation(wts[:, 1], wts[:, 1], ACT.Exp).then_inc(we_ready[r], 1)
                with act.Fori(0, GROUPS // 2) as i:
                    for u in range(2):
                        g = i * 2 + u
                        act.wait_ge(hot_used[r], g + 1)
                        act.wait_ge(hi_ready[r], g + 1)
                        for c in range(TOPK):
                            ins = act.activation(hot_en[:, u, c, :, 0, :], hot_hi[:, u, c], ACT.Copy,
                                                 scale=C["entry_p"][:, c:c + 1])
                        ins.then_inc(en_ready[r], 1)
                with act.Fori(0, SGROUPS) as G:
                    for c in range(FC):
                        act.wait_ge(h_ready[r], G * FC + (c + 1))
                        act.activation(hid[:, c], bank[1 + c], ACT.Gelu).then_inc(gelu_done[r], 1)
            ffn(1)

            act.dma_start(markf[0:1, :], a["c_mark"][:, 0:1]).then_inc(mark_in, 16)
            act.wait_ge(mark_in, 16)
            act.wait_ge(fills, 5)
            act.activation(pT[0:1, 0, :].bitcast(BF16)[:, 0:P], zeros[0:1, 0:P], ACT.Identity, bias=markf[0:1, :])\
                .then_inc(mark_made, 1)
            act.wait_ge(mark_made, 1)
            for hh in range(HB):
                act.dma_start(kb[KROWS:KR1, 0, hh * P:(hh + 1) * P], pT[0:1, 0, :].bitcast(BF16)[:, 0:P]).then_inc(mark_in, 16)
            act.wait_ge(mark_in, 16 * (HB + 1))
            act.sem_inc(mark_ready, 1)

            def project(g, u):
                if have(g, 0):
                    copy_xT(2, g, u)
                if have(g, 1):
                    hold(v_ready, g + 2)
                    act.activation(
                        vE[:, bass.ds((g - 1) * GT + 1, GT), :].rearrange("p t (h c) -> p (t h) c", c=VW)[:, :, 0:HDB],
                        bank[6 + (1 - u)].rearrange("p (th c) -> p th c", c=HDB), ACT.Copy).then_inc(v_copied, 1)
                if have(g, 2):
                    for m in range(2):
                        act.wait_ge(rest1, g * 2 + m - 3)
                        act.activation(part[u][:, m, 1], qk[:, u, m], ACT.Copy).then_inc(part2, 1)
                if have(g, 1):
                    for m in range(2):
                        act.wait_ge(parts_free, g)
                        act.wait_ge(qk_ready, g * 2 + m - 1)
                        act.activation(part[1 - u][:, m, 0], qk[:, 1 - u, m], ACT.Copy).then_inc(part1, 1)

            act.sem_inc(v_copied, 2)
            by_group(act, project, 2)

            def slot(g, s):
                g0, s0, there = step_at(g, s, OT_LAG)
                if there and s0 % NQUAD == 0:
                    j = s0 // NQUAD
                    act.wait_ge(oT_ready, g0 * GT + j + 1)
                    act.activation(oT[:, j % 2], bank[6 + j % 2][:, 0:P], ACT.Copy).then_inc(oT_copied, 1)
                g0, s0, there = step_at(g, s, TURN_LAG)
                if there:
                    act.wait_ge(pT_ready, g0 * STEPS + s0 + 1)
                    act.activation(pT[:, s0 % LANES], bank[4 + s0 % 2], ACT.Copy).then_inc(pT_copied, 1)
                g0, s0, there = step_at(g, s, 0)
                if there:
                    for k in range(QUAD):
                        if k % 2 == 0:
                            act.wait_ge(nm_ready, g0 * (2 * STEPS) + (2 * s0 + k // 2 + 1))
                        ins = act.activation(pb[:, s0 % LANES, k, :], ps_s[s0 % 2][:, 2 * k * P:(2 * k + 1) * P], ACT.Exp,
                                             bias=nm[:, s0 % 2, k:k + 1])
                        if k % 2 == 1:
                            ins.then_inc(p_ready, 1)

            slots(act, slot)
            ffn(3)

        @block.vector
        def _(dve):
            chains = iter(dve_chain)

            def new_chain():
                return Chain(dve, next(chains))

            def hold(s, value):
                dve.wait_ge(s, value)
                dve.sem_inc(spacer["dve"], 1)

            def stats(ch, src, i):
                for j in range(2 * GT):
                    ch.did(dve.bn_stats(stat6[:, j, :], flat(src[:, tile(i * 2 * GT + j), :])))
                ch.settle()
                dve.sem_inc(spacer["dve"], 1)
                for j in range(2 * GT):
                    ch.did(dve.bn_aggr(mv[:, j, :], stat6[:, j, :]))
                ch.settle()
                cols = bass.ds(i * 2 * GT, 2 * GT)
                ch.did(dve.tensor_scalar(mean[:, cols], mv[:, :, 0], 1.0, None, ALU.mult))
                ch.did(dve.tensor_scalar(vareps[:, cols], mv[:, :, 1], EPS, None, ALU.add))

            def make_rstd(ch):
                ch.settle()
                ch.did(dve.tensor_scalar(seed[:], vareps[:].bitcast(I32), 1, None, ALU.logical_shift_right))
                ch.settle()
                ch.did(dve.tensor_scalar(rstd[:].bitcast(I32), seed[:], -1.0, float(0x5F3759DF), ALU.mult, ALU.add))
                ch.settle()
                for _ in range(4):
                    ch.did(dve.tensor_tensor(root[:], rstd[:], rstd[:], ALU.mult))
                    ch.settle()
                    ch.did(dve.scalar_tensor_tensor(root[:], root[:], -0.5, vareps[:], ALU.mult, ALU.mult))
                    ch.settle()
                    ch.did(dve.scalar_tensor_tensor(rstd[:], root[:], 1.5, rstd[:], ALU.add, ALU.mult))
                    ch.settle()

            def norm(r, post, lag):
                def body(g, u):
                    if have(g, 0):
                        if later(g):
                            dve.wait_ge(xT_ready[r], g + 1)
                            if r == 0:
                                dve.wait_ge(h_kept, g - 1)
                            if r in (1, 3):
                                dve.wait_ge(xn_out[r][u], out_count(g, u))
                        for j in range(GT):
                            t = g * GT + j
                            ins = dve.tensor_scalar(xn[:, u, j, :], flat(x[:, tile(t), :]), mean[:, tile(t)],
                                                    rstd[:, tile(t)], ALU.subtract, ALU.mult)
                        ins.then_inc(xn_ready[r], 1)
                    if have(g, lag):
                        post(g - lag, (u - lag) % 2)

                def out_count(g, u):
                    return g * 8 - 8 * u

                by_group(dve, body, lag)

            dve.wait_ge(consts_made, 5)
            dve.wait_ge(const_in, 16 * NCONST)
            dve.tensor_copy(before_bf[:], C["before"][:]).then_inc(consts_made, 1)
            dve.tensor_scalar(attpad[:, GROUPS * HA - HA:GROUPS * HA], C["head_of"][:], attr[:, 0:1], None, ALU.mult)\
                .then_inc(consts_made, 1)

            ch = new_chain()
            for half in range(2):
                dve.wait_ge(x_in[half], 16)
                with dve.Fori(half * GROUPS // 4, (half + 1) * GROUPS // 4) as i:
                    with ch.turn(i, 18):
                        stats(ch, x, i)
            ch.after(GROUPS // 2, 18)
            make_rstd(ch)

            def leaky_part(G, u):
                dve.wait_ge(sr_done, G + 1)
                dve.wait_ge(fr_ready, G + 3)
                dve.tensor_scalar(leaky[:, u], bank[2 + u], 0.01, None, ALU.mult).then_inc(fr_scaled, 1)
                dve.wait_ge(fr_scaled, G + 1)
                dve.tensor_tensor(leaky[:, u], leaky[:, u], bank[2 + u], ALU.max).then_inc(leaky_ready, 1)

            norm(0, leaky_part, 1)
            dve.wait_ge(sr_done, GROUPS + 2)
            dve.tensor_reduce(nmax[0:HAB, :], bank[4][0:HAB, :], AX_X, ALU.max, negate=True).then_inc(a_dve, 1)
            dve.wait_ge(a_act, 1)
            ch.did(dve.reciprocal(prec[0:HAB, :], psum_row[0:HAB, :]))
            ch.settle()
            dve.tensor_scalar(pa[0:HAB, :], pa[0:HAB, :], prec[0:HAB, 0:1], None, ALU.mult).then_inc(a_dve, 1)
            dve.wait_ge(a_pe, 3)
            ch.did(dve.tensor_tensor(ctxm[:].rearrange("p (b h) -> p b h", h=HA),
                                     bank[7][:, 0:HAB].rearrange("p (b h) -> p b h", h=HA),
                                     C["head_of"][:].unsqueeze(1).broadcast_to([P, GROUPS, HA]), ALU.mult))
            ch.settle()
            dve.tensor_reduce(ctxT[:], ctxm[:].rearrange("p (b h) -> p b h", h=HA), AX_X, ALU.add).then_inc(a_dve, 1)
            dve.wait_ge(a_act, 5)
            dve.wait_ge(h_kept, GROUPS)
            ch = new_chain()
            with dve.Fori(0, GROUPS // 2) as i:
                with ch.turn(i, 20):
                    for u in range(2):
                        g = i * 2 + u
                        hg = h[:, bass.ds(g * GT, GT), :]
                        ch.did(dve.tensor_tensor(hg, hg, fh[:, tile(g), :].broadcast_to([P, GT, D]), ALU.add))
                    ch.settle()
                    dve.sem_inc(spacer["dve"], 1)
                    stats(ch, h, i)
            ch.after(GROUPS // 2, 20)
            make_rstd(ch)
            dve.wait_ge(beta_added, 1)
            ch = new_chain()
            with dve.Fori(0, GROUPS // 2) as i:
                with ch.turn(i, 16):
                    for u in range(2):
                        g = i * 2 + u
                        for j in range(GT):
                            t = g * GT + j
                            ch.did(dve.scalar_tensor_tensor(upd[:, u, j, :], flat(h[:, tile(t), :]), mean[:, tile(t)],
                                                            gamma[:], ALU.subtract, ALU.mult))
                    ch.settle()
                    for u in range(2):
                        g = i * 2 + u
                        for j in range(GT):
                            t = g * GT + j
                            ch.did(dve.scalar_tensor_tensor(flat(x[:, tile(t), :]), upd[:, u, j, :], rstd[:, tile(t)],
                                                            flat(x[:, tile(t), :]), ALU.mult, ALU.add))
                    ch.settle()
            ch.after(GROUPS // 2, 16)

            def all_stats():
                ch = new_chain()
                with dve.Fori(0, GROUPS // 2) as i:
                    with ch.turn(i, 18):
                        stats(ch, x, i)
                ch.after(GROUPS // 2, 18)
                make_rstd(ch)

            def bc(ap, n):
                return ap.unsqueeze(2).broadcast_to([P, TILES, n])

            def order():
                return C["order"][:].unsqueeze(1).broadcast_to([P, TILES, E])

            def ffn(r):
                all_stats()

                def keep_logits(G, u):
                    dve.wait_ge(lg_ready[r], G + 3)
                    dve.tensor_scalar(lg[:, bass.ds(G * GT, GT), :],
                                      bank[2 + u].rearrange("p (t e) -> p t e", t=GT)[:, :, 0:E], 1.0, None, ALU.mult)\
                        .then_inc(lg_read[r], 1)

                norm(r, keep_logits, 2)
                ch = new_chain()
                dve.wait_ge(lg_read[r], GROUPS + 2)
                for c in range(TOPK):
                    ch.did(dve.tensor_reduce(top[:, c], lg[:], AX_X, ALU.max))
                    ch.settle()
                    ch.did(dve.tensor_tensor(pick[:], lg[:], bc(top[:, c], E), ALU.is_equal))
                    ch.settle()
                    ch.did(dve.tensor_tensor(pick[:], pick[:], order(), ALU.mult))
                    ch.settle()
                    ch.did(dve.tensor_reduce(best[:], pick[:], AX_X, ALU.max))
                    ch.settle()
                    ch.did(dve.tensor_tensor(hot[:, c], order(), bc(best[:], E), ALU.is_equal))
                    ch.settle()
                    if c == 0:
                        ch.did(dve.scalar_tensor_tensor(lg[:], hot[:, 0], -3.0e38, lg[:], ALU.mult, ALU.add))
                        ch.settle()
                dve.tensor_tensor(took[:].rearrange("p (t e) -> p t e", e=E), hot[:, 0], hot[:, 1], ALU.add)\
                    .then_inc(took_ready[r], 1)
                dve.tensor_tensor(wts[:, 1], top[:, 1], top[:, 0], ALU.subtract).then_inc(wd_ready[r], 1)
                dve.wait_ge(rank_ready[r], 1)
                ch.did(dve.tensor_copy(tot[:], bank[5][:, 0:TILES * E].rearrange("p (t e) -> p e t", e=E)))
                ch.settle()
                ch.did(dve.tensor_tensor_scan(incl[:].rearrange("p e t -> p (e t)"), onesf[:],
                                              tot[:].rearrange("p e t -> p (e t)"), 0.0, ALU.mult, ALU.add))
                ch.settle()
                ch.did(dve.tensor_tensor(incl[:], incl[:], tot[:], ALU.subtract))
                ch.settle()
                ch.did(dve.tensor_tensor(posf[:], bank[4][:, 0:TILES * E].rearrange("p (t e) -> p t e", e=E),
                                         incl[:].rearrange("p e t -> p t e"), ALU.add))
                ch.settle()
                for c in range(TOPK):
                    ch.did(dve.tensor_tensor(pick[:], hot[:, c], posf[:], ALU.mult))
                    ch.settle()
                    ch.did(dve.tensor_reduce(pos[:, c], pick[:], AX_X, ALU.add))
                    ch.settle()
                ch.did(dve.tensor_copy(pos_i[:, 0], pos[:].rearrange("p k t -> p (k t)")))
                ch.settle()
                ch.did(dve.tensor_scalar(pos_i[:, 1], pos_i[:, 0], P - 1, None, ALU.bitwise_and))
                ch.settle()
                ch.did(dve.tensor_scalar(pos_i[:, 0], pos_i[:, 0], 7, None, ALU.logical_shift_right))
                ch.settle()
                ch.did(dve.tensor_copy(pos_hl[:], pos_i[:]))
                ch.settle()
                dve.wait_ge(we_ready[r], 1)
                ch.did(dve.tensor_scalar(den[:], wts[:, 1], 1.0, None, ALU.add))
                ch.settle()
                ch.did(dve.reciprocal(wts[:, 0], den[:]))
                ch.settle()
                ch.did(dve.tensor_tensor(wts[:, 1], wts[:, 1], wts[:, 0], ALU.mult))
                with dve.Fori(0, GROUPS // 2) as i:
                    for u in range(2):
                        g = i * 2 + u
                        at = bass.ds(g * GT, GT)

                        def place(part, n):
                            v = pos_hl[:, part].rearrange("p (k t) -> p k t", k=TOPK)[:, :, at]
                            return v.unsqueeze(3).broadcast_to([P, TOPK, GT, n])

                        def count(n):
                            return C["iota"][:, 0:n].unsqueeze(1).unsqueeze(1).broadcast_to([P, TOPK, GT, n])

                        dve.wait_ge(hot_used[r], g + 1)
                        dve.tensor_tensor(hot_hi[:, u], count(ST), place(0, ST), ALU.is_equal).then_inc(hi_ready[r], 1)
                        dve.tensor_tensor(hot_lo[:, u], count(P), place(1, P), ALU.is_equal).then_inc(hot_ready[r], 1)
                dve.wait_ge(hot_used[r], GROUPS + 2)
                ch.did(dve.tensor_copy(entry_pt[:], bank[6][:, 0:2 * ST]))
                ch.settle()
                ch.did(dve.scalar_tensor_tensor(entry_i[:], entry_pt[:, ST:2 * ST], float(TOPK * P), entry_pt[:, 0:ST],
                                                ALU.mult, ALU.add))
                ch.settle()
                dve.tensor_scalar(token_i[:], entry_i[:], 1, None, ALU.logical_shift_right).then_inc(index_ready[r], 1)

                def copy_x(G, u):
                    dve.wait_ge(xgT_ready[r], G + 5)
                    dve.tensor_copy(xs[:, u], bank[0]).then_inc(xs_ready[r], 1)

                def copy_y(G, k):
                    dve.wait_ge(ys_free[r], G + 1)
                    dve.wait_ge(y_ready[r], G + 1)
                    dve.tensor_copy(ys[:, k].rearrange("p a d -> p (a d)"), bank[5 + k % 2]).then_inc(ys_ready[r], 1)

                copy_x(0, 0)

                def turn(i, last):
                    for k in range(4):
                        G = i * 4 + k
                        if not (last and k == 3):
                            copy_x(G + 1, (k + 1) % 2)
                        copy_y(G, k)

                with dve.Fori(0, SGROUPS // 4 - 1) as i:
                    turn(i, False)
                turn(SGROUPS // 4 - 1, True)

                ch = new_chain()
                dve.sem_inc(x_done[r], 2)
                with dve.Fori(0, GROUPS // 2) as i:
                    with ch.turn(i, 8):
                        for u in range(2):
                            g = i * 2 + u
                            dve.wait_ge(yb_in[r][u], i * 16 + 16)
                            for j in range(GT):
                                t = g * GT + j
                                ch.did(dve.scalar_tensor_tensor(upd[:, u, j, :], yb[:, u, j, 0:D], wts[:, 0, tile(t)],
                                                                flat(x[:, tile(t), :]), ALU.mult, ALU.add))
                            ch.settle()
                            for j in range(GT):
                                t = g * GT + j
                                ins = dve.scalar_tensor_tensor(flat(x[:, tile(t), :]), yb[:, u, j, D:2 * D],
                                                               wts[:, 1, tile(t)], upd[:, u, j, :], ALU.mult, ALU.add)
                            ins.then_inc(x_done[r], 1)
                dve.wait_ge(x_done[r], GROUPS + 2)

            ffn(1)

            all_stats()

            def rotate(G, u):
                if not isinstance(G, int) or G > 0:
                    dve.wait_ge(qk_ready, G * 2)
                for m, (cos, sin) in enumerate((("cosq", "sinq"), ("cosk", "sink"))):
                    for c, tab in enumerate((cos, sin)):
                        dve.wait_ge(proj_ready, G * 4 + 2 * m + c + 1)
                        dve.tensor_tensor(rot[:, m, c], bank[2 + 2 * m + c], C[tab][:], ALU.mult).then_inc(rot_ready, 1)
                dve.wait_ge(part3, G * 2 + 2)
                for m in range(2):
                    dve.wait_ge(rot_ready, G * 4 + 2 * m + 6)
                    dve.tensor_tensor(qk[:, u, m], rot[:, m, 0], rot[:, m, 1], ALU.add).then_inc(qk_ready, 1)

            dve.sem_inc(rot_ready, 4)
            norm(2, rotate, 1)

            def softmax(g, s):
                par = s % 2
                sc = ps_s[par][:].rearrange("p (k w j) -> p k w j", w=2, j=P)
                for half in range(2):
                    hold(s_ready, g * (2 * STEPS) + (2 * s + half + 1))
                    pair = sc[:, 2 * half:2 * half + 2]
                    dve.copy_predicated(pair[:, :, 0, :], causal[:].unsqueeze(1).broadcast_to([P, 2, P]), pair[:, :, 1, :])\
                        .then_inc(merged, 1)
                for half in range(2):
                    dve.wait_ge(merged, g * (2 * STEPS) + (2 * s + half + 1))
                    dve.tensor_reduce(nm[:, par, 2 * half:2 * half + 2], sc[:, 2 * half:2 * half + 2, 0, :], AX_X, ALU.max,
                                      negate=True).then_inc(nm_ready, 1)

            def take_out(g, j):
                dve.wait_ge(pv_done, (g * GT + j + 3) * NQUAD)
                dve.tensor_copy(oS[:, j % 2], bank[6 + j % 2]).then_inc(oS_ready, 1)

            def normalise(g, j):
                o = bank[6 + j % 2].rearrange("p (h c) -> p h c", c=VC)
                dve.wait_ge(oq_ready, g * GT + j + 1)
                dve.reciprocal(rden[:, j % 2].unsqueeze(2), o[:, :, HDB:VW]).then_inc(rden_ready, 1)
                dve.wait_ge(rden_ready, g * GT + j + 1)
                dve.tensor_tensor(ob[:, j % 2].rearrange("p (h c) -> p h c", c=HDB), o[:, :, 0:HDB],
                                  rden[:, j % 2].unsqueeze(2).broadcast_to([P, HB, HDB]), ALU.mult).then_inc(o_ready, 1)

            def add_out(g, j):
                t = g * GT + j
                dve.wait_ge(wo_done, t + 1)
                dve.tensor_tensor(flat(x[:, tile(t), :]), flat(x[:, tile(t), :]), bank[6 + j % 2][:, P:2 * P], ALU.add)\
                    .then_inc(x_added, 1)

            def slot(g, s):
                for lag, do in ((TAKE_LAG, take_out), (NORM_LAG, normalise), (ADD_LAG, add_out)):
                    g0, s0, there = step_at(g, s, lag)
                    if there and s0 % NQUAD == 0:
                        do(g0, s0 // NQUAD)
                g0, s0, there = step_at(g, s, 0)
                if there:
                    softmax(g0, s0)

            dve.wait_ge(bo_added, 1)
            slots(dve, slot)
            dve.wait_ge(x_added, TILES + 2)
            ffn(3)

        @block.tensor
        def _(pe):
            ident = C["ident"]
            pe.wait_ge(const_in, 16 * NCONST)
            pe.wait_ge(consts_made, 7)

            def transposed(r, g, u):
                if later(g):
                    pe.wait_ge(xnT_ready[r], g - 1)
                pe.wait_ge(xn_ready[r], g + 1)
                for j in range(GT):
                    ins = pe.transpose(bank[u][:, j * P:(j + 1) * P], xn[:, u, j, :], ident[:])
                ins.then_inc(xT_ready[r], 1)

            pe.sem_inc(xT_ready[0], 2)
            pe.sem_inc(fr_ready, 2)
            pe.matmul(bank[4][0:HAB, :], zeros[:, 0:HAB], zeros[:, :], start=True, stop=True)
            pe.sem_inc(sr_done, 2)

            def additive(g, u):
                if have(g, 0):
                    transposed(0, g, u)
                if have(g, 1):
                    pe.wait_ge(xnT_ready[0], g)
                    pe.matmul(bank[2 + (1 - u)], W["WrT"][:], xnT[:, 1 - u], start=True, stop=True).then_inc(fr_ready, 1)
                if have(g, 2):
                    pe.wait_ge(attb_ready, g - 1)
                    pe.wait_ge(leaky_ready, g - 1)
                    pe.matmul(bank[4][0:HAB, :], attb[:, u], leaky[:, u], start=False, stop=True,
                              skip_group_check=True).then_inc(sr_done, 1)

            by_group(pe, additive, 2)
            pe.wait_ge(a_dve, 2)
            for j in range(GT):
                ins = pe.transpose(bank[5][:, j * HAB:(j + 1) * HAB], pa[0:HAB, j * P:(j + 1) * P], ident[0:HAB, 0:HAB])
            ins.then_inc(a_pe, 1)
            pe.wait_ge(a_act, 2)
            pe.wait_ge(h_kept, GROUPS)
            for b in range(GROUPS):
                for j in range(GT):
                    ins = pe.matmul(bank[6][:, b * HA:(b + 1) * HA], h[:, b * GT + j, :],
                                    paT[:, j * HAB + b * HA:j * HAB + (b + 1) * HA], start=(j == 0), stop=(j == GT - 1))
            ins.then_inc(a_pe, 1)
            pe.wait_ge(a_act, 3)
            pe.matmul(bank[7][:, 0:HAB], W["WrT"][:], GT_sb[:], start=True, stop=True).then_inc(a_pe, 1)
            pe.wait_ge(a_dve, 3)
            for b in range(GROUPS):
                ins = pe.matmul(bank[b // GT][:, b % GT * D:(b % GT + 1) * D], ctxT[:, b:b + 1].broadcast_to([P, P]),
                                W["WfT"][:], start=True, stop=True)
                if b % GT == GT - 1:
                    ins.then_inc(a_pe, 1)

            def ffn(r):
                pe.sem_inc(xT_ready[r], 2)
                pe.sem_inc(lg_ready[r], 2)
                pe.sem_inc(lg_read[r], 2)

                def logits(g, u):
                    if have(g, 0):
                        transposed(r, g, u)
                    if have(g, 1):
                        pe.wait_ge(xnT_ready[r], g)
                        pe.wait_ge(lg_read[r], g)
                        for j in range(GT):
                            ins = pe.matmul(bank[2 + (1 - u)][:, j * P:(j + 1) * P], xnT[:, 1 - u, j * P:(j + 1) * P],
                                            rwT[:], start=True, stop=True)
                        ins.then_inc(lg_ready[r], 1)

                by_group(pe, logits, 1)
                pe.wait_ge(took_ready[r], 1)
                pe.matmul(bank[4][:, 0:TILES * E], before_bf[:], took[:], start=True, stop=True)
                pe.matmul(bank[5][:, 0:TILES * E], ones_bf[:], took[:], start=True, stop=True).then_inc(rank_ready[r], 1)
                pe.matmul(bank[6][:, 0:2 * ST], zeros[:, 0:P], zeros[:, 0:2 * ST], start=True, stop=True)
                pe.sem_inc(hot_used[r], 2)
                with pe.Fori(0, GROUPS // 2) as i:
                    for u in range(2):
                        g = i * 2 + u
                        for s in (hot_ready[r], en_ready[r], ent_ready[r]):
                            pe.wait_ge(s, g + 1)
                        for c in range(TOPK):
                            for j in range(GT):
                                ins = pe.matmul(bank[6][:, 0:2 * ST], hot_lo[:, u, c, j],
                                                hot_en[:, u, c, j].rearrange("p a b -> p (a b)"),
                                                start=False, stop=True, skip_group_check=True)
                        ins.then_inc(hot_used[r], 1)

                def turn_tokens(i, k):
                    pe.wait_ge(g_in[r][k], i * (16 * SGT) + 16 * SGT)
                    for j in range(SGT):
                        ins = pe.transpose(bank[0][:, j * P:(j + 1) * P], xg[:, k, j, :], ident[:])
                    ins.then_inc(xgT_ready[r], 1)

                pe.sem_inc(xgT_ready[r], 4)
                turn_tokens(0, 0)

                def turn(i, last):
                    for k in range(4):
                        G, u = i * 4 + k, k // 2
                        if k % 2 == 0:
                            pe.wait_ge(w_in[r][u], i * 32 + 32)
                        pe.wait_ge(xs_ready[r], G + 1)
                        for c in range(FC):
                            pe.matmul(bank[1 + c], w1b[:, u, c * P:(c + 1) * P], xs[:, k % 2], start=True, stop=True)\
                                .then_inc(h_ready[r], 1)
                        if not (last and k == 3):
                            turn_tokens(i + (k + 1) // 4, (k + 1) % 4)
                        for j in range(SGT):
                            for c in range(FC):
                                if j == 0:
                                    pe.wait_ge(gelu_done[r], G * FC + (c + 1))
                                ins = pe.matmul(bank[5 + k % 2][:, j * D:(j + 1) * D], hid[:, c, j * P:(j + 1) * P],
                                                w2b[:, u, c, :], start=(c == 0), stop=(c == FC - 1))
                        ins.then_inc(y_ready[r], 1)

                with pe.Fori(0, SGROUPS // 4 - 1) as i:
                    turn(i, False)
                turn(SGROUPS // 4 - 1, True)

            ffn(1)

            pe.sem_inc(xT_ready[2], 2)
            pe.sem_inc(v_ready, 2)

            def projections(g, u):
                if have(g, 0):
                    transposed(2, g, u)
                if have(g, 1):
                    G, v = g - 1, 1 - u
                    pe.wait_ge(xnT_ready[2], g)
                    for m, k in enumerate(("WqT", "WqrT", "WkT", "WkrT")):
                        pe.wait_ge(rot_ready, G * 4 + m + 1)
                        pe.matmul(bank[2 + m], W[k][:], xnT[:, v], start=True, stop=True).then_inc(proj_ready, 1)
                    pe.wait_ge(v_copied, G + 1)
                    for j in range(GT):
                        ins = pe.matmul(bank[6 + v][:, j * D:(j + 1) * D], xnT[:, v, j * P:(j + 1) * P], W["WvT"][:],
                                        start=True, stop=True)
                    ins.then_inc(v_ready, 1)

            by_group(pe, projections, 1)

            def scores(g, s):
                j, q = divmod(s, NQUAD)
                if q == 0:
                    pe.wait_ge(qk_in[j], g * (16 * 2 * PARTS) + 16 * 2 * PARTS)
                for k in range(QUAD):
                    if k % 2 == 0 and (not isinstance(g, int) or g * STEPS + s >= 2):
                        pe.wait_ge(p_ready, g * (2 * STEPS) + (2 * s + k // 2 - 3))
                    hc = slice((q * QUAD + k) * P, (q * QUAD + k + 1) * P)
                    ins = pe.matmul(ps_s[s % 2][:, 2 * k * P:(2 * k + 2) * P].rearrange("p (w j) -> p w j", j=P),
                                    qb[0:KR1, j, hc], kb[0:KR1, j:j + 2, hc], start=True, stop=True)
                    if k % 2 == 1:
                        ins.then_inc(s_ready, 1)

            def turn_weights(g, s):
                if not isinstance(g, int) or g * STEPS + s >= 2:
                    pe.wait_ge(pT_copied, g * STEPS + (s - 1))
                pe.wait_ge(p_ready, g * (2 * STEPS) + (2 * s + 2))
                for k in range(QUAD):
                    ins = pe.transpose(bank[4 + s % 2][:, k * P:(k + 1) * P], pb[:, s % LANES, k, :], ident[:])
                ins.then_inc(pT_ready, 1)

            def weigh(g, s):
                j, q = divmod(s, NQUAD)
                if q == 0:
                    pe.wait_ge(vt_ready, (g * GT + j) * 2 + 2)
                    pe.wait_ge(x_added, g * GT + j + 1)
                pe.wait_ge(pTc_ready, g * STEPS + s + 1)
                for share, v in ((pT, vp), (pTc, vd)):
                    for k in range(QUAD):
                        ins = pe.matmul(bank[6 + j % 2][k * VC:(k + 1) * VC, q * P:(q + 1) * P],
                                        v[:, j % 2, q * QUAD + k, :], share[:, s % LANES, k * P:(k + 1) * P],
                                        start=share is pT, stop=share is pTc, tile_position=(0, k * VC))
                ins.then_inc(pv_done, 1)

            def turn_results(g, j):
                pe.wait_ge(oS_ready, g * GT + j + 1)
                for q in range(NQUAD):
                    ins = pe.transpose(bank[6 + j % 2][:, q * P:(q + 1) * P], oS[:, j % 2, q * P:(q + 1) * P], ident[:])
                ins.then_inc(oq_ready, 1)

            def turn_out(g, j):
                pe.wait_ge(o_ready, g * GT + j + 1)
                pe.transpose(bank[6 + j % 2][:, 0:P], ob[:, j % 2], ident[:]).then_inc(oT_ready, 1)

            def project(g, j):
                pe.wait_ge(oT_copied, g * GT + j + 1)
                pe.matmul(bank[6 + j % 2][:, P:2 * P], oT[:, j % 2], W["WoT"][:], start=True, stop=True).then_inc(wo_done, 1)

            pe.sem_inc(pv_done, 2 * NQUAD)
            pe.sem_inc(x_added, 2)
            pe.wait_ge(v_copied, GROUPS + 2)
            pe.wait_ge(rot_ready, 4 * GROUPS + 4)

            def slot(g, s):
                for lag, do in ((0, scores), (TURN_LAG, turn_weights), (WEIGH_LAG, weigh)):
                    g0, s0, there = step_at(g, s, lag)
                    if there:
                        do(g0, s0)
                for lag, do in ((TURN_RES_LAG, turn_results), (TURN_OUT_LAG, turn_out), (PROJ_LAG, project)):
                    g0, s0, there = step_at(g, s, lag)
                    if there and s0 % NQUAD == 0:
                        do(g0, s0 // NQUAD)

            slots(pe, slot)
            ffn(3)


def kernel(**inputs):
    import concourse.bacc as bacc
    from concourse.bass_utils import run_bass_kernel_spmd

    nc = bacc.Bacc("TRN2", target_bir_lowering=False, num_devices=1)
    i = {k: np.ascontiguousarray(v) for k, v in inputs.items()}
    rows = np.arange(D).reshape(HB, HDB)
    swap = rows.reshape(HB, 2, HDB // 2)[:, ::-1].reshape(HB, HDB).T.reshape(-1)
    rows = rows.T.reshape(-1)
    arrays = {
        "x": i["L0_attn_a_h"].reshape(B * N, D),
        "WrT": i["L0_attn_a_Wr"].T, "WfT": i["L0_attn_a_Wf"].T,
        "WqT": i["L0_attn_b_Wq"][rows].T, "WqrT": i["L0_attn_b_Wq"][swap].T,
        "WkT": i["L0_attn_b_Wk"][rows].T, "WkrT": i["L0_attn_b_Wk"][swap].T,
        "WvT": i["L0_attn_b_Wv"].T, "WoT": i["L0_attn_b_Wo"].T,
        "rwT": i["L0_ffn_router_w"].T,
        "attr": np.tile(i["L0_attn_a_att_r"].reshape(HDA), HA).reshape(D, 1),
        "gamma": i["L0_attn_a_ln_gamma"].reshape(1, D), "beta": i["L0_attn_a_ln_beta"].reshape(1, D),
        "bo": i["L0_attn_b_bo"].reshape(1, D),
        "w1": i["L0_ffn_w1"], "w2": i["L0_ffn_w2"],
    }
    arrays.update({"c_" + k: v for k, v in tables().items()})
    arrays = {"in_" + k: np.ascontiguousarray(v) for k, v in arrays.items()}
    aps = {k[3:]: nc.dram_tensor(k, v.shape, mybir.dt.from_np(v.dtype), kind="ExternalInput").ap()
           for k, v in arrays.items()}
    out = nc.dram_tensor("out_dram", (B * N, D), F32, kind="ExternalOutput").ap()
    hybrid_block(nc, aps, out)
    r = run_bass_kernel_spmd(nc, [arrays], core_ids=[0])
    return r.results[0]["out_dram"].reshape(B, N, D)
```

```python
from contextlib import ExitStack, contextmanager

import numpy as np

import concourse.bass as bass
from concourse import mybir

P = 128
D = 128
B, N = 8, 512
TILES = B * N // P
GT = N // P
GROUPS = TILES // GT
HA = 8
HDA = D // HA
HB = 16
HDB = D // HB
E = 8
FF = 512
FC = FF // P
TOPK = 2
SLOTS = B * N * TOPK
SGT = 4
SG = SGT * P
SGROUPS = SLOTS // SG
ST = SLOTS // P
EPS = 1e-5
PARTS = 3
KROWS = PARTS * PARTS * HDB
KR1 = KROWS + 1
QUAD = 4
NQUAD = HB // QUAD
STEPS = GT * NQUAD
VW = HDB + 1
VC = 32
LANES = 4
NEG = -1.0e30

F32 = mybir.dt.float32
BF16 = mybir.dt.bfloat16
I32 = mybir.dt.int32
ALU = mybir.AluOpType
ACT = mybir.ActivationFunctionType
AX_X = mybir.AxisListType.X


class Chain:

    def __init__(self, eng, sem):
        self.eng, self.sem, self.base, self.n = eng, sem, 0, 0

    def did(self, ins):
        ins.then_inc(self.sem, 1)
        self.n += 1

    def settle(self):
        self.eng.wait_ge(self.sem, self.base + self.n)

    @contextmanager
    def turn(self, i, per):
        start, self.base = self.n, i * per
        yield
        assert self.n - start == per, (self.n - start, per)
        self.n = start

    def after(self, turns, per):
        self.base, self.n = 0, self.n + turns * per


def step_at(g, s, lag):
    q, r = divmod(s - lag, STEPS)
    return g + q, r, not isinstance(g, int) or 0 <= g + q < GROUPS


def tables():
    p, t, k = np.arange(P), np.arange(TILES), np.arange(TOPK)
    f = np.float32
    c = {}
    c["ident"] = np.eye(P, dtype=f)
    c["before"] = (p[:, None] < p[None, :]).astype(f)
    c["iota"] = np.tile(np.arange(P, dtype=f), (P, 1))
    c["entry_p"] = (TOPK * p[:, None] + k[None, :]).astype(f)
    c["entry_t"] = np.tile(t.astype(f), (P, 1))
    c["order"] = np.tile((E - np.arange(E)).astype(f), (P, 1))
    c["head_of"] = (p[:, None] // HDA == np.arange(HA)[None, :]).astype(f)
    c["causal"] = (p[None, :] <= p[:, None]).astype(np.int32)
    c["causal_t"] = (p[:, None] <= p[None, :]).astype(f)
    inv = (f(1.0) / np.power(f(10000.0), np.arange(0, HDB, 2, dtype=f) / f(HDB))).astype(f)
    ang = np.arange(N, dtype=f)[:, None] * inv[None, :]
    ang = np.concatenate([ang, ang], -1).T.astype(f)
    sign = np.where(np.arange(HDB) < HDB // 2, -1.0, 1.0)[:, None]
    cos, sin = np.cos(ang.astype(np.float64)), np.sin(ang.astype(np.float64)) * sign
    for name, s in (("q", HDB ** -0.5), ("k", 1.0)):
        c["cos" + name] = np.repeat(cos * s, HB, 0).astype(f)
        c["sin" + name] = np.repeat(sin * s, HB, 0).astype(f)
    return c


def hybrid_block(nc, a, out):
    with ExitStack() as ctx:
        def sb(name, shape, dt=F32):
            return ctx.enter_context(nc.sbuf_tensor("sb_" + name, shape, dt))

        def sem(name):
            return ctx.enter_context(nc.semaphore(name))

        def sems(name, n):
            return [sem(f"{name}{k}") for k in range(n)]

        def psum(name, cols):
            return ctx.enter_context(nc.psum_tensor(name, [P, cols], F32))

        ps_s = [psum("ps_s0", 1024), psum("ps_s1", 1024)]
        bank = [ps_s[0][:, 0:512], ps_s[0][:, 512:1024], ps_s[1][:, 0:512], ps_s[1][:, 512:1024]]
        bank += [psum(f"bank{k}", 512)[:, :] for k in range(4, 8)]

        c_shapes = {"ident": P, "before": P, "iota": P, "entry_p": TOPK, "entry_t": TILES, "order": E, "head_of": HA,
                    "causal_t": P, "cosq": N, "sinq": N, "cosk": N, "sink": N}
        C = {k: sb("c_" + k, [P, w]) for k, w in c_shapes.items()}
        causal = sb("causal", [P, P], I32)
        W = {k: sb(k, [P, D]) for k in ("WrT", "WfT", "WqT", "WqrT", "WkT", "WkrT", "WvT", "WoT")}
        rwT = sb("rwT", [P, P])
        attr = sb("attr", [P, 1])
        gamma = sb("gamma", [P, D])
        beta = sb("beta", [P, D])
        bo = sb("bo", [P, D])
        zeros = sb("zeros", [P, 512])
        ones_bf = sb("ones_bf", [P, P], BF16)
        before_bf = sb("before_bf", [P, P], BF16)

        x = sb("x", [P, TILES, D])
        mean = sb("mean", [P, TILES])
        vareps = sb("vareps", [P, TILES])
        rstd = sb("rstd", [P, TILES])
        root = sb("root", [P, TILES])
        seed = sb("seed", [P, TILES], I32)
        stat6 = sb("stat6", [P, TILES, 6])
        halves = sb("halves", [P, 3, TILES])
        negms = sb("negms", [P, TILES])
        xn = sb("xn", [P, 2, GT, D])
        xnT = sb("xnT", [P, 2, GT * P])
        upd = sb("upd", [P, 2, GT, D])

        h = sb("h", [P, TILES, D])
        leaky = sb("leaky", [P, 2, N])
        attpad = sb("attpad", [P, 2 * GROUPS * HA])
        attb = sb("attb", [P, 2, GROUPS * HA])
        HAB = GROUPS * HA
        nmax = sb("nmax", [P, 1])
        psum_row = sb("psum_row", [P, 1])
        prec = sb("prec", [P, 1])
        pa = sb("pa", [P, N])
        paT = sb("paT", [P, GT * HAB + VC])
        G_sb = sb("G_sb", [P, 2, D])
        GT_sb = sb("GT_sb", [P, HAB])
        ctxm = sb("ctxm", [P, HAB])
        ctxT = sb("ctxT", [P, GROUPS])
        fh = sb("fh", [P, GROUPS, D])

        lg = sb("lg", [P, TILES, E])
        top = sb("top", [P, TOPK, TILES])
        pick = sb("pick", [P, TOPK, TILES, E])
        best = sb("best", [P, TILES])
        hot = sb("hot", [P, TOPK, TILES, E])
        wts = sb("wts", [P, TOPK, TILES])
        den = sb("den", [P, TILES])
        took = sb("took", [P, TILES * E], BF16)
        onesf = sb("onesf", [P, E * TILES])
        upto = sb("upto", [P, 1 + E * TILES])
        posf = sb("posf", [P, TILES, E])
        pos = sb("pos", [P, TOPK, TILES])
        pos_i = sb("pos_i", [P, 2, TOPK * TILES], I32)
        pos_hl = sb("pos_hl", [P, 2, TOPK * TILES])
        hot_lo = sb("hot_lo", [P, 2, TOPK, GT, P], BF16)
        hot_hi = sb("hot_hi", [P, 2, TOPK, GT, ST], BF16)
        hot_en = sb("hot_en", [P, 2, TOPK, GT, 2, ST], BF16)
        entry_pt = sb("entry_pt", [P, 2 * ST])
        entry_i = sb("entry_i", [P, ST], I32)
        token_i = sb("token_i", [P, ST], I32)

        w1b = sb("w1b", [P, 2, FF])
        w2b = sb("w2b", [P, 2, FC, D])
        tcol = sb("tcol", [P, 4, SGT], I32)
        ecol = sb("ecol", [P, 4, SGT], I32)
        results = sb("results", [P, 4 * 4 * SG])
        quarter = [results[:, k * 4 * SG:(k + 1) * 4 * SG] for k in range(4)]
        yb = results[:].rearrange("p (g t c) -> p g t c", t=GT, c=TOPK * D)
        xg = quarter[0].rearrange("p (k j d) -> p k j d", j=SGT, d=D)
        xs = sb("xs", [P, 2, SG])
        hid = quarter[1].rearrange("p (c s) -> p c s", s=SG)
        ys = quarter[2].rearrange("p (k j d) -> p k j d", j=SGT, d=D)

        rot = hid.rearrange("p (m c) n -> p m c n", m=2)
        qk = quarter[3].rearrange("p (u m n) -> p u m n", m=2, n=N)
        part = [quarter[k].bitcast(BF16)[:, 0:2 * PARTS * N].rearrange("p (m c n) -> p m c n", m=2, c=PARTS)
                for k in (0, 2)]
        vE = sb("vE", [P, TILES + 1, HB * VW])
        qb = h[:].rearrange("p t d -> p (t d)").bitcast(BF16).rearrange("p (j c) -> p j c", j=GT)
        kb = sb("kb", [P, GT + 1, HB * P], BF16)
        nm = sb("nm", [P, 2, QUAD])
        pb = quarter[1].rearrange("p (b k j) -> p b k j", b=LANES, j=P)
        pT = quarter[3].rearrange("p (b c) -> p b c", b=LANES)
        pTc = quarter[0].rearrange("p (b c) -> p b c", b=LANES)
        vp = sb("vp", [P, 2, HB, VC])
        vd = sb("vd", [P, 2, HB, VC])
        oS = sb("oS", [P, 2, NQUAD * P])
        rden = sb("rden", [P, 2, HB])
        ob = sb("ob", [P, 2, D])
        oT = sb("oT", [P, 2, P])
        mark = sb("mark", [P, P], BF16)

        def dram(name, shape, dt=F32):
            return nc.dram_tensor(name, shape, dt).ap()

        xn_dram = [dram(f"xn_dram{r}", (B * N, D)) for r in range(2)]
        y_dram = [dram(f"y_dram{r}", (SLOTS, D)) for r in range(2)]
        qk_dram = dram("qk_dram", (TILES, 2, PARTS, HDB, HB, P), BF16)

        const_in = sem("const_in")
        x_in = sems("x_in", 2)
        consts_made = sem("consts_made")
        act_chain = sem("act_chain")
        dve_chain = [sem(f"dve_chain{k}") for k in range(12)]
        spacer = {e: sem("spacer_" + e) for e in ("pool", "act", "dve")}
        xn_ready = sems("xn_ready", 4)
        h_kept = {r: sem(f"h_kept{r}") for r in (0, 1, 3)}
        xn_out = {r: sem(f"xn_out{r}") for r in (1, 3)}
        xT_ready = sems("xT_ready", 4)
        xnT_ready = sems("xnT_ready", 4)

        fr_ready = sem("fr_ready")
        fr_scaled = sem("fr_scaled")
        fills = sem("fills")
        leaky_ready = sem("leaky_ready")
        sr_done = sem("sr_done")
        attb_ready = sem("attb_ready")
        a_pe = sem("a_pe")
        a_act = sem("a_act")
        a_dve = sem("a_dve")
        beta_added = sem("beta_added")
        y_summed = sem("y_summed")
        y_normed = sem("y_normed")
        y_scaled = sem("y_scaled")
        y_added = sem("y_added")
        share_ready = {r: sem(f"share_ready{r}") for r in (1, 3)}
        share_added = {r: sem(f"share_added{r}") for r in (1, 3)}

        lg_ready = {r: sem(f"lg_ready{r}") for r in (1, 3)}
        lg_read = {r: sem(f"lg_read{r}") for r in (1, 3)}
        took_ready = {r: sem(f"took_ready{r}") for r in (1, 3)}
        rank_ready = {r: sem(f"rank_ready{r}") for r in (1, 3)}
        hi_ready = {r: sem(f"hi_ready{r}") for r in (1, 3)}
        en_ready = {r: sem(f"en_ready{r}") for r in (1, 3)}
        ent_ready = {r: sem(f"ent_ready{r}") for r in (1, 3)}
        hot_ready = {r: sem(f"hot_ready{r}") for r in (1, 3)}
        hot_used = {r: sem(f"hot_used{r}") for r in (1, 3)}
        wd_ready = {r: sem(f"wd_ready{r}") for r in (1, 3)}
        we_ready = {r: sem(f"we_ready{r}") for r in (1, 3)}
        columns_ready = {r: sem(f"columns_ready{r}") for r in (1, 3)}
        w_in = sems("w_in", 2)
        index_made = {r: sem(f"index_made{r}") for r in (1, 3)}
        g_in = {r: sems(f"g_in{r}_", 4) for r in (1, 3)}
        xgT_ready = {r: sem(f"xgT_ready{r}") for r in (1, 3)}
        xs_ready = {r: sem(f"xs_ready{r}") for r in (1, 3)}
        h_ready = {r: sem(f"h_ready{r}") for r in (1, 3)}
        gelu_done = {r: sem(f"gelu_done{r}") for r in (1, 3)}
        y_ready = {r: sem(f"y_ready{r}") for r in (1, 3)}
        ys_ready = {r: sem(f"ys_ready{r}") for r in (1, 3)}
        ys_free = {r: sem(f"ys_free{r}") for r in (1, 3)}
        y_out = {r: sems(f"y_out{r}_", 4) for r in (1, 3)}
        YB_CUTS = ((0, 1), (1, 2), (2, 4), (4, 6), (6, GROUPS))
        yb_in = sems("yb_in", len(YB_CUTS))
        yb_ready = {r: sem(f"yb_ready{r}") for r in (1, 3)}
        x_done = {r: sem(f"x_done{r}") for r in (1, 3)}

        proj_ready = sem("proj_ready")
        rot_ready = sem("rot_ready")
        qk_ready = sem("qk_ready")
        part1 = sem("part1")
        rest1 = sem("rest1")
        part2 = sem("part2")
        part3 = sem("part3")
        parts_out = sems("parts_out", 2)
        v_ready = sem("v_ready")
        v_copied = sem("v_copied")
        bo_added = sem("bo_added")
        mark_in = sem("mark_in")
        qk_in = sems("qk_in", GT)
        s_ready = sem("s_ready")
        merged = sem("merged")
        rden_ready = sem("rden_ready")
        nm_ready = sem("nm_ready")
        p_ready = sem("p_ready")
        pT_ready = sem("pT_ready")
        pT_copied = sem("pT_copied")
        pTc_ready = sem("pTc_ready")
        vt_ready = sem("vt_ready")
        pv_done = sem("pv_done")
        oS_ready = sem("oS_ready")
        oq_ready = sem("oq_ready")
        o_ready = sem("o_ready")
        x_added = sem("x_added")
        oT_ready = sem("oT_ready")
        oT_copied = sem("oT_copied")
        wo_done = sem("wo_done")
        out_done = sem("out_done")

        xnT_read = {0: fr_ready, 1: lg_ready[1], 2: v_ready, 3: lg_ready[3]}

        block = ctx.enter_context(nc.Block())
        NCONST = len(C) + 1 + len(W) + 5

        def by_group(eng, body, tail, first=2):
            for g in range(first):
                body(g, g % 2)
            with eng.Fori(first // 2, GROUPS // 2) as i:
                for u in range(2):
                    body(i * 2 + u, u)
            for g in range(GROUPS, GROUPS + tail):
                body(g, g % 2)

        def have(g, lag):
            return not isinstance(g, int) or 0 <= g - lag < GROUPS

        def later(g):
            return not isinstance(g, int) or g >= 2

        def tile(t):
            return bass.ds(t, 1)

        TURN_LAG, WEIGH_LAG = 2, 5
        TAKE_LAG, TURN_RES_LAG, NORM_LAG, TURN_OUT_LAG, OT_LAG, PROJ_LAG, ADD_LAG, STATS_LAG = 9, 9, 11, 11, 12, 12, 13, 14

        def slots(eng, slot):
            for s in range(STEPS):
                slot(0, s)
            with eng.Fori(1, GROUPS) as g:
                for s in range(STEPS):
                    slot(g, s)
            for s in range(STATS_LAG + 1):
                slot(GROUPS, s)

        def flat(ap):
            return ap.rearrange("p a d -> p (a d)")

        @block.sync
        def _(sp):
            xt = a["x"].rearrange("(t p) d -> p t d", p=P)
            for half in range(2):
                s = slice(half * TILES // 2, (half + 1) * TILES // 2)
                sp.dma_start(x[:, s, :], xt[:, s, :]).then_inc(x_in[half], 16)
            for k in C:
                sp.dma_start(C[k][:], a["c_" + k]).then_inc(const_in, 16)
            sp.dma_start(causal[:], a["c_causal"]).then_inc(const_in, 16)
            for k in W:
                sp.dma_start(W[k][:], a[k]).then_inc(const_in, 16)
            sp.dma_start(rwT[:, 0:E], a["rwT"]).then_inc(const_in, 16)
            sp.dma_start(attr[:], a["attr"]).then_inc(const_in, 16)
            for dst, k in ((gamma, "gamma"), (beta, "beta"), (bo, "bo")):
                sp.dma_start(dst[:], a[k].broadcast_to([P, D])).then_inc(const_in, 16)

            def ffn(r):
                n = r // 2
                rows = xn_dram[n].rearrange("(t p) d -> p t d", p=P)
                with sp.Fori(0, GROUPS) as g:
                    sp.wait_ge(h_kept[r], g + 1)
                    sp.dma_start(rows[:, bass.ds(g * GT, GT), :], h[:, bass.ds(g * GT, GT), :]).then_inc(xn_out[r], 16)
                sp.sem_inc(ys_free[r], 4)
                w1r = a["w1"].rearrange("e d f -> d e f")
                w2r = a["w2"].rearrange("e (c f) d -> f e c d", f=P)

                def load_expert(e, u):
                    sp.dma_start(w1b[:, u], flat(w1r[:, tile(e), :])).then_inc(w_in[u], 16)
                    sp.dma_start(w2b[:, u], w2r[:, tile(e)].rearrange("f e c d -> f (e c) d")).then_inc(w_in[u], 16)

                def turn(i, load):
                    for k in range(4):
                        sp.wait_ge(y_out[r][k], i * (16 * SGT) + 16 * SGT)
                        sp.sem_inc(ys_free[r], 1)
                        if k % 2 == 1 and load:
                            sp.wait_ge(y_ready[r], i * 4 + k + 1)
                            load_expert((i * 2 + 2 + k // 2) % E, k // 2)

                if r == 1:
                    for u in range(2):
                        load_expert(u, u)
                with sp.Fori(0, SGROUPS // 4 - 1) as i:
                    turn(i, True)
                turn(SGROUPS // 4 - 1, r == 1)
                yr = y_dram[n].rearrange("(t p k) d -> p t (k d)", p=P, k=TOPK)
                for c, (g0, g1) in enumerate(YB_CUTS):
                    sp.dma_start(yb[:, g0:g1].rearrange("p g t c -> p (g t) c"), yr[:, GT * g0:GT * g1, :])\
                        .then_inc(yb_in[c], 16)
                for c, (g0, g1) in enumerate(YB_CUTS):
                    sp.wait_ge(yb_in[c], 16 * (n + 1))
                    sp.sem_inc(yb_ready[r], g1 - g0)

            ffn(1)

            def store_parts(i, u):
                sp.wait_ge(part3, i * 4 + (2 * u + 6))
                for j in range(GT):
                    dst = qk_dram[tile((i * 2 + u) * GT + j)].rearrange("t m c d h n -> (d h) (t m c) n")
                    sp.dma_start(dst, part[u][:, :, :, j * P:(j + 1) * P].rearrange("p m c n -> p (m c) n"))\
                        .then_inc(parts_out[u], 16)

            def load_qk(g, j):
                t = g * GT + j
                qsrc = qk_dram[tile(t), 0].rearrange("t a d h n -> t (a d) (h n)")
                sp.dma_start(qb[0:KROWS, j], qsrc.broadcast_to([PARTS, PARTS * HDB, HB * P])).then_inc(qk_in[j], 16)
                for c in range(PARTS):
                    ksrc = qk_dram[tile(t), 1, c].rearrange("t d h n -> t d (h n)")
                    sp.dma_start(kb[c * PARTS * HDB:(c + 1) * PARTS * HDB, j + 1],
                                 ksrc.broadcast_to([PARTS, HDB, HB * P])).then_inc(qk_in[j], 16)

            sp.wait_ge(fills, 5)
            sp.dma_start(kb[KROWS:KR1, 0, :].rearrange("r (h p) -> r h p", p=P),
                         mark[0:1, :].unsqueeze(1).broadcast_to([1, HB, P])).then_inc(mark_in, 16)
            sp.wait_ge(fills, 6)
            sp.wait_ge(mark_in, 16)
            store_parts(0, 0)
            store_parts(0, 1)
            sp.wait_ge(parts_out[0], 16 * GT)
            for i in range(1, GROUPS // 2):
                for u in range(2):
                    if i > 1:
                        load_qk(0, (i - 2) * 2 + u)
                    store_parts(i, u)
            for u in range(2):
                sp.wait_ge(parts_out[u], 16 * GT * (GROUPS // 2))
            with sp.Fori(1, GROUPS) as g:
                for j in range(GT):
                    sp.wait_ge(s_ready, (g - 1) * (2 * STEPS) + 2 * min(j + 2, GT) * NQUAD)
                    load_qk(g, j)

            ffn(3)
            ot = out.rearrange("(t p) d -> p t d", p=P)
            with sp.Fori(0, GROUPS) as g:
                sp.wait_ge(x_done[3], g + 1)
                sp.dma_start(ot[:, bass.ds(g * GT, GT), :], x[:, bass.ds(g * GT, GT), :]).then_inc(out_done, 16)
            sp.wait_ge(out_done, 16 * GROUPS)

        @block.gpsimd
        def _(pool):
            def hold(s, value):
                pool.wait_ge(s, value)
                pool.sem_inc(spacer["pool"], 1)

            pool.memset(rwT[:, E:P], 0.0).then_inc(consts_made, 1)
            pool.memset(zeros[:], 0.0).then_inc(consts_made, 1)
            pool.memset(ones_bf[:], 1.0).then_inc(consts_made, 1)
            pool.memset(onesf[:], 1.0).then_inc(consts_made, 1)
            pool.memset(upto[:, 0:1], 0.0).then_inc(consts_made, 1)
            pool.memset(attpad[:], 0.0).then_inc(consts_made, 1)
            pool.memset(paT[:, GT * HAB:], 0.0).then_inc(consts_made, 1)

            pool.memset(mark[0:1, :], NEG).then_inc(fills, 1)
            pool.memset(kb[:], 0.0).then_inc(fills, 1)
            pool.memset(vE[:], 1.0).then_inc(fills, 1)
            pool.memset(vp[:], 0.0).then_inc(fills, 1)
            pool.memset(vd[:], 0.0).then_inc(fills, 1)

            pool.wait_ge(consts_made, 9)
            pool.wait_ge(const_in, 16 * NCONST)
            with pool.Fori(0, GROUPS // 2) as i:
                for u in range(2):
                    g = i * 2 + u
                    hold(sr_done, g + 1)
                    pool.tensor_copy(attb[:, u], attpad[:, bass.ds(GROUPS * HA - HA - g * HA, GROUPS * HA)])\
                        .then_inc(attb_ready, 1)
            pool.tensor_tensor(x[:], x[:], beta[:].unsqueeze(1).broadcast_to([P, TILES, D]), ALU.add)\
                .then_inc(beta_added, 1)

            pool.wait_ge(a_act, 6)
            with pool.Fori(0, GROUPS) as g:
                hg = h[:, bass.ds(g * GT, GT), :]
                pool.tensor_tensor(hg, hg, fh[:, tile(g), :].broadcast_to([P, GT, D]), ALU.add).then_inc(y_summed, 1)
            with pool.Fori(0, GROUPS) as g:
                hg = h[:, bass.ds(g * GT, GT), :]
                hold(y_normed, g + 1)
                pool.tensor_tensor(hg, hg, gamma[:].unsqueeze(1).broadcast_to([P, GT, D]), ALU.mult).then_inc(y_scaled, 1)

            def ffn(r):
                n = r // 2
                with pool.Fori(0, GROUPS // 2) as i:
                    for u in range(2):
                        g = i * 2 + u
                        hold(hot_used[r], g + 1)
                        hold(hi_ready[r], g + 1)
                        pool.tensor_tensor(
                            hot_en[:, u, :, :, 1, :], hot_hi[:, u],
                            C["entry_t"][:, bass.ds(g * GT, GT)].unsqueeze(1).unsqueeze(3)
                            .broadcast_to([P, TOPK, GT, ST]), ALU.mult).then_inc(ent_ready[r], 1)
                def gather(k):
                    for j in range(SGT):
                        pool.indirect_dma_start(xg[:, k, j, :], None, xn_dram[n],
                                                bass.IndirectOffsetOnAxis(ap=tcol[:, k, j:j + 1], axis=0))\
                            .then_inc(g_in[r][k], 16)

                def scatter(k):
                    for j in range(SGT):
                        pool.indirect_dma_start(y_dram[n], bass.IndirectOffsetOnAxis(ap=ecol[:, k, j:j + 1], axis=0),
                                                ys[:, k, j, :], None).then_inc(y_out[r][k], 16)

                pool.wait_ge(xn_out[r], 16 * GROUPS)
                for k in range(2):
                    pool.wait_ge(columns_ready[r], k + 1)
                    gather(k)

                def turn(i, last):
                    for k in range(4):
                        G = i * 4 + k
                        if not (last and k >= 2):
                            k2 = (k + 2) % 4
                            hold(xgT_ready[r], G + 3)
                            hold(columns_ready[r], G + 3)
                            gather(k2)
                        hold(ys_ready[r], G + 1)
                        scatter(k)

                turns = SGROUPS // 4
                with pool.Fori(0, turns - 1) as i:
                    turn(i, False)
                turn(turns - 1, True)
                for k in range(4):
                    pool.wait_ge(y_out[r][k], 16 * SGT * turns)
                with pool.Fori(0, GROUPS // 2) as i:
                    for u in range(2):
                        g = i * 2 + u
                        xs_g = x[:, bass.ds(g * GT, GT), :]
                        hold(share_ready[r], g + 1)
                        pool.tensor_tensor(xs_g, xs_g, upd[:, u], ALU.add).then_inc(share_added[r], 1)
            ffn(1)
            pool.memset(qb, 1.0).then_inc(fills, 1)

            pool.sem_inc(part3, 4)

            def rests(g, u):
                if have(g, 1):
                    for m in range(2):
                        pool.wait_ge(part2, g * 2 + m - 1)
                        pool.tensor_tensor(part[1 - u][:, m, 2], qk[:, 1 - u, m], part[1 - u][:, m, 1], ALU.subtract)\
                            .then_inc(part3, 1)
                if have(g, 0):
                    for m in range(2):
                        pool.wait_ge(part1, g * 2 + m + 1)
                        pool.tensor_tensor(qk[:, u, m], qk[:, u, m], part[u][:, m, 0], ALU.subtract).then_inc(rest1, 1)

            by_group(pool, rests, 1)
            pool.wait_ge(v_copied, GROUPS + 2)
            def heads(v):
                return v.rearrange("p t (h c) -> p (t h) c", c=VW)

            def values(g, j):
                t = g * GT + j
                hold(pv_done, (t + 1) * NQUAD)
                pool.tensor_copy(vp[:, j % 2, :, 0:VW], heads(vE[:, tile(t), :])).then_inc(vt_ready, 1)
                pool.tensor_tensor(vd[:, j % 2, :, 0:VW], heads(vE[:, tile(t + 1), :]), heads(vE[:, tile(t), :]),
                                   ALU.subtract).then_inc(vt_ready, 1)

            pool.wait_ge(parts_out[0], 16 * GT * (GROUPS // 2))
            with pool.Fori(0, GROUPS) as g:
                for s in range(STEPS):
                    if s % NQUAD == 0:
                        values(g, s // NQUAD)
                    pool.wait_ge(pT_copied, g * STEPS + s + 1)
                    pool.tensor_tensor(pTc[:, s % LANES].rearrange("p (k q) -> p k q", q=P),
                                       pT[:, s % LANES].rearrange("p (k q) -> p k q", q=P),
                                       C["causal_t"][:].unsqueeze(1).broadcast_to([P, QUAD, P]), ALU.mult)\
                        .then_inc(pTc_ready, 1)

            ffn(3)

        @block.scalar
        def _(act):
            ch = Chain(act, act_chain)

            def hold(s, value):
                act.wait_ge(s, value)
                act.sem_inc(spacer["act"], 1)

            def copy_xn(r, g, u):
                if r != 2:
                    hold(xn_ready[r], g + 1)
                    act.activation(h[:, bass.ds(g * GT, GT), :].rearrange("p t d -> p (t d)"),
                                   xn[:, u].rearrange("p t d -> p (t d)"), ACT.Copy).then_inc(h_kept[r], 1)
                act.wait_ge(xnT_read[r], g + 1)
                act.wait_ge(xT_ready[r], g + 3)
                act.activation(xnT[:, u], bank[u], ACT.Copy).then_inc(xnT_ready[r], 1)

            def additive(g, u):
                if have(g, 0):
                    copy_xn(0, g, u)
                if have(g, 1):
                    hold(sr_done, g)
                    hold(fr_ready, g + 2)
                    act.activation(leaky[:, 1 - u], bank[2 + (1 - u)], ACT.Copy, scale=0.01).then_inc(fr_scaled, 1)

            by_group(act, additive, 1)
            act.wait_ge(a_dve, 1)
            act.activation(pa[0:HAB, :], bank[4][0:HAB, :], ACT.Exp, bias=nmax[0:HAB, :],
                           accum_out=psum_row[0:HAB, :]).then_inc(a_act, 1)
            act.wait_ge(a_pe, 1)
            act.activation(paT[:, 0:GT * HAB], bank[5][:, 0:GT * HAB], ACT.Copy).then_inc(a_act, 1)
            act.wait_ge(a_pe, 2)
            act.activation(G_sb[:].rearrange("p b d -> p (b d)"), bank[6][:, 0:2 * D], ACT.Copy).then_inc(a_act, 1)
            act.wait_ge(a_pe, 3)
            act.activation(GT_sb[:].rearrange("p (b h) -> p b h", h=HA),
                           bank[5][:, 0:2 * P].rearrange("p (b c) -> p b c", c=VC)[:, :, 0:HA], ACT.Copy).then_inc(a_act, 1)
            for b in range(2):
                act.wait_ge(a_pe, 5 + b)
                act.activation(fh[:, b * GT:(b + 1) * GT, :].rearrange("p a d -> p (a d)"), bank[b], ACT.Copy)\
                    .then_inc(a_act, 1)
            act.wait_ge(a_dve, 4)
            with act.Fori(0, GROUPS) as g:
                for j in range(GT):
                    t = g * GT + j
                    ins = act.activation(flat(h[:, tile(t), :]), flat(h[:, tile(t), :]), ACT.Identity,
                                         bias=negms[:, tile(t)], scale=rstd[:, tile(t)])
                ins.then_inc(y_normed, 1)

            def ffn(r):
                with act.Fori(0, GROUPS // 2) as i:
                    for u in range(2):
                        copy_xn(r, i * 2 + u, u)
                act.wait_ge(wd_ready[r], 1)
                act.activation(wts[:, 1], wts[:, 1], ACT.Exp).then_inc(we_ready[r], 1)
                with act.Fori(0, GROUPS // 2) as i:
                    for u in range(2):
                        g = i * 2 + u
                        act.wait_ge(hot_used[r], g + 1)
                        act.wait_ge(hi_ready[r], g + 1)
                        for c in range(TOPK):
                            ins = act.activation(hot_en[:, u, c, :, 0, :], hot_hi[:, u, c], ACT.Copy,
                                                 scale=C["entry_p"][:, c:c + 1])
                        ins.then_inc(en_ready[r], 1)
                with act.Fori(0, SGROUPS) as G:
                    for c in range(FC):
                        act.wait_ge(h_ready[r], G * FC + (c + 1))
                        act.activation(hid[:, c], bank[1 + c], ACT.Gelu).then_inc(gelu_done[r], 1)
                act.sem_inc(share_added[r], 2)
                with act.Fori(0, GROUPS // 2) as i:
                    for u in range(2):
                        g = i * 2 + u
                        hold(share_added[r], g + 1)
                        hold(yb_ready[r], g + 1)
                        for j in range(GT):
                            ins = act.activation(upd[:, u, j, :], flat(yb[:, tile(g), j, 0:D]), ACT.Copy,
                                                 scale=wts[:, 0, tile(g * GT + j)])
                        ins.then_inc(share_ready[r], 1)
            ffn(1)

            def project(g, u):
                if have(g, 0):
                    copy_xn(2, g, u)
                if have(g, 1):
                    hold(v_ready, g + 2)
                    act.activation(
                        vE[:, bass.ds((g - 1) * GT + 1, GT), :].rearrange("p t (h c) -> p (t h) c", c=VW)[:, :, 0:HDB],
                        bank[6 + (1 - u)].rearrange("p (th c) -> p th c", c=HDB), ACT.Copy).then_inc(v_copied, 1)
                if have(g, 2):
                    for m in range(2):
                        act.wait_ge(rest1, g * 2 + m - 3)
                        act.activation(part[u][:, m, 1], qk[:, u, m], ACT.Copy).then_inc(part2, 1)
                if have(g, 1):
                    G, v = g - 1, 1 - u
                    if later(G):
                        act.wait_ge(parts_out[v], G * (8 * GT) - 8 * GT * v)
                    for m in range(2):
                        act.wait_ge(qk_ready, g * 2 + m - 1)
                        act.activation(part[1 - u][:, m, 0], qk[:, 1 - u, m], ACT.Copy).then_inc(part1, 1)

            act.sem_inc(v_copied, 2)
            by_group(act, project, 2, first=4)
            act.wait_ge(qk_ready, 2 * GROUPS)

            def slot(g, s):
                g0, s0, there = step_at(g, s, OT_LAG)
                if there and s0 % NQUAD == 0:
                    j = s0 // NQUAD
                    act.wait_ge(oT_ready, g0 * GT + j + 1)
                    act.activation(oT[:, j % 2], bank[6 + j % 2][:, 0:P], ACT.Copy).then_inc(oT_copied, 1)
                g0, s0, there = step_at(g, s, TURN_LAG)
                if there:
                    if isinstance(g, int) and (g, s) == (0, TURN_LAG):
                        act.wait_ge(part3, 2 * GROUPS + 4)
                    act.wait_ge(pT_ready, g0 * STEPS + s0 + 1)
                    act.activation(pT[:, s0 % LANES], bank[4 + s0 % 2], ACT.Copy).then_inc(pT_copied, 1)
                g0, s0, there = step_at(g, s, 0)
                if there:
                    for k in range(QUAD):
                        if k % 2 == 0:
                            act.wait_ge(nm_ready, g0 * (2 * STEPS) + (2 * s0 + k // 2 + 1))
                        ins = act.activation(pb[:, s0 % LANES, k, :], ps_s[s0 % 2][:, 2 * k * P:(2 * k + 1) * P], ACT.Exp,
                                             bias=nm[:, s0 % 2, k:k + 1])
                        if k % 2 == 1:
                            ins.then_inc(p_ready, 1)

            slots(act, slot)
            ffn(3)

        @block.vector
        def _(dve):
            chains = iter(dve_chain)

            def new_chain():
                return Chain(dve, next(chains))

            def hold(s, value):
                dve.wait_ge(s, value)
                dve.sem_inc(spacer["dve"], 1)

            def stats(ch, src, g):
                for j in range(GT):
                    t = g * GT + j
                    ch.did(dve.bn_stats(flat(stat6[:, tile(t), :]), flat(src[:, tile(t), :])))

            def group_stats(g, ready, value, done):
                hold(ready, value)
                for j in range(GT):
                    t = g * GT + j
                    ins = dve.bn_stats(flat(stat6[:, tile(t), :]), flat(x[:, tile(t), :]))
                ins.then_inc(done, 1)

            def make_mean(ch):
                ch.settle()
                even, odd = stat6[:, :, 0:3], stat6[:, :, 3:6]
                ch.did(dve.tensor_tensor(halves[:, 0], even[:, :, 1], odd[:, :, 1], ALU.add))
                ch.did(dve.tensor_tensor(halves[:, 1], even[:, :, 1], odd[:, :, 1], ALU.subtract))
                ch.did(dve.tensor_tensor(halves[:, 2], even[:, :, 2], odd[:, :, 2], ALU.add))
                ch.settle()
                ch.did(dve.tensor_scalar(mean[:], halves[:, 0], 0.5, None, ALU.mult))
                ch.did(dve.scalar_tensor_tensor(root[:], halves[:, 1], 0.25, halves[:, 1], ALU.mult, ALU.mult))
                ch.did(dve.tensor_scalar(vareps[:], halves[:, 2], 1.0 / D, EPS, ALU.mult, ALU.add))
                ch.settle()
                ch.did(dve.tensor_tensor(vareps[:], vareps[:], root[:], ALU.add))

            def make_rstd(ch):
                make_mean(ch)
                ch.settle()
                ch.did(dve.tensor_scalar(seed[:], vareps[:].bitcast(I32), 1, None, ALU.logical_shift_right))
                ch.settle()
                ch.did(dve.tensor_scalar(rstd[:].bitcast(I32), seed[:], -1.0, float(0x5F3759DF), ALU.mult, ALU.add))
                ch.settle()
                for _ in range(3):
                    ch.did(dve.tensor_tensor(root[:], rstd[:], rstd[:], ALU.mult))
                    ch.settle()
                    ch.did(dve.scalar_tensor_tensor(root[:], root[:], -0.5, vareps[:], ALU.mult, ALU.mult))
                    ch.settle()
                    ch.did(dve.scalar_tensor_tensor(rstd[:], root[:], 1.5, rstd[:], ALU.add, ALU.mult))
                    ch.settle()

            def norm(r, post, lag):
                def body(g, u):
                    if have(g, 0):
                        if later(g):
                            dve.wait_ge(xT_ready[r], g + 1)
                            if r != 2:
                                dve.wait_ge(h_kept[r], g - 1)
                        for j in range(GT):
                            t = g * GT + j
                            ins = dve.tensor_scalar(xn[:, u, j, :], flat(x[:, tile(t), :]), mean[:, tile(t)],
                                                    rstd[:, tile(t)], ALU.subtract, ALU.mult)
                        ins.then_inc(xn_ready[r], 1)
                    if have(g, lag):
                        post(g - lag, (u - lag) % 2)

                by_group(dve, body, lag)

            ch = new_chain()
            for g in range(GROUPS):
                if g % (GROUPS // 2) == 0:
                    dve.wait_ge(x_in[g // (GROUPS // 2)], 16)
                stats(ch, x, g)
            make_rstd(ch)
            dve.wait_ge(consts_made, 7)
            dve.wait_ge(const_in, 16 * NCONST)
            dve.tensor_copy(before_bf[:], C["before"][:]).then_inc(consts_made, 1)
            dve.tensor_scalar(attpad[:, GROUPS * HA - HA:GROUPS * HA], C["head_of"][:], attr[:, 0:1], None, ALU.mult)\
                .then_inc(consts_made, 1)

            def leaky_part(G, u):
                dve.wait_ge(fr_scaled, G + 1)
                dve.tensor_tensor(leaky[:, u], leaky[:, u], bank[2 + u], ALU.max).then_inc(leaky_ready, 1)

            norm(0, leaky_part, 2)
            dve.wait_ge(sr_done, GROUPS + 2)
            dve.tensor_reduce(nmax[0:HAB, :], bank[4][0:HAB, :], AX_X, ALU.max, negate=True).then_inc(a_dve, 1)
            dve.wait_ge(a_act, 1)
            ch.did(dve.reciprocal(prec[0:HAB, :], psum_row[0:HAB, :]))
            ch.settle()
            dve.tensor_scalar(pa[0:HAB, :], pa[0:HAB, :], prec[0:HAB, 0:1], None, ALU.mult).then_inc(a_dve, 1)
            dve.wait_ge(a_pe, 4)
            ch.did(dve.tensor_tensor(ctxm[:].rearrange("p (b h) -> p b h", h=HA),
                                     bank[7][:, 0:HAB].rearrange("p (b h) -> p b h", h=HA),
                                     C["head_of"][:].unsqueeze(1).broadcast_to([P, GROUPS, HA]), ALU.mult))
            ch.settle()
            dve.tensor_reduce(ctxT[:], ctxm[:].rearrange("p (b h) -> p b h", h=HA), AX_X, ALU.add).then_inc(a_dve, 1)
            ch = new_chain()
            with dve.Fori(0, GROUPS // 4) as i:
                with ch.turn(i, 4 * GT):
                    for u in range(4):
                        hold(y_summed, i * 4 + (u + 1))
                        stats(ch, h, i * 4 + u)
            ch.after(GROUPS // 4, 4 * GT)
            make_rstd(ch)
            dve.scalar_tensor_tensor(negms[:], mean[:], -1.0, rstd[:], ALU.mult, ALU.mult).then_inc(a_dve, 1)
            dve.wait_ge(beta_added, 1)
            ch = new_chain()

            def add_y(g, u):
                if have(g, 0):
                    x_g, y_g = (v[:, bass.ds(g * GT, GT), :] for v in (x, h))
                    dve.wait_ge(y_scaled, g + 1)
                    dve.tensor_tensor(x_g, x_g, y_g, ALU.add).then_inc(y_added, 1)
                if have(g, 1):
                    group_stats(g - 1, y_added, g, ch.sem)

            by_group(dve, add_y, 1)
            ch.after(GROUPS, 1)

            def bc(ap, n):
                return ap.unsqueeze(2).broadcast_to([P, TILES, n])

            def order():
                return C["order"][:].unsqueeze(1).broadcast_to([P, TILES, E])

            def ffn(r, ch):
                make_rstd(ch)

                def keep_logits(G, u):
                    dve.wait_ge(lg_ready[r], G + 3)
                    dve.tensor_scalar(lg[:, bass.ds(G * GT, GT), :],
                                      bank[2 + u].rearrange("p (t e) -> p t e", t=GT)[:, :, 0:E], 1.0, None, ALU.mult)\
                        .then_inc(lg_read[r], 1)

                norm(r, keep_logits, 2)
                ch = new_chain()
                dve.wait_ge(lg_read[r], GROUPS + 2)
                for c in range(TOPK):
                    ch.did(dve.tensor_reduce(top[:, c], lg[:], AX_X, ALU.max))
                    ch.settle()
                    ch.did(dve.tensor_tensor(pick[:, 0], lg[:], bc(top[:, c], E), ALU.is_equal))
                    ch.settle()
                    ch.did(dve.tensor_tensor(pick[:, 0], pick[:, 0], order(), ALU.mult))
                    ch.settle()
                    ch.did(dve.tensor_reduce(best[:], pick[:, 0], AX_X, ALU.max))
                    ch.settle()
                    ch.did(dve.tensor_tensor(hot[:, c], order(), bc(best[:], E), ALU.is_equal))
                    ch.settle()
                    if c == 0:
                        ch.did(dve.scalar_tensor_tensor(lg[:], hot[:, 0], -3.0e38, lg[:], ALU.mult, ALU.add))
                        ch.settle()
                dve.tensor_tensor(took[:].rearrange("p (t e) -> p t e", e=E), hot[:, 0], hot[:, 1], ALU.add)\
                    .then_inc(took_ready[r], 1)
                dve.tensor_tensor(wts[:, 1], top[:, 1], top[:, 0], ALU.subtract).then_inc(wd_ready[r], 1)
                dve.wait_ge(rank_ready[r], 1)
                ch.did(dve.tensor_tensor_scan(upto[:, 1:], onesf[:], bank[5][:, 0:TILES * E], 0.0, ALU.mult, ALU.add))
                ch.settle()
                before = upto[:, 0:TILES * E].rearrange("p (e t) -> p t e", e=E)
                ch.did(dve.tensor_tensor(posf[:], bank[4][:, 0:TILES * E].rearrange("p (t e) -> p t e", e=E), before,
                                         ALU.add))
                ch.settle()
                ch.did(dve.tensor_tensor(pick[:], hot[:], posf[:].unsqueeze(1).broadcast_to([P, TOPK, TILES, E]),
                                         ALU.mult))
                ch.settle()
                ch.did(dve.tensor_reduce(pos[:].rearrange("p k t -> p (k t)"),
                                         pick[:].rearrange("p k t e -> p (k t) e"), AX_X, ALU.add))
                ch.settle()
                ch.did(dve.tensor_copy(pos_i[:, 0], pos[:].rearrange("p k t -> p (k t)")))
                ch.settle()
                ch.did(dve.tensor_scalar(pos_i[:, 1], pos_i[:, 0], P - 1, None, ALU.bitwise_and))
                ch.settle()
                ch.did(dve.tensor_scalar(pos_i[:, 0], pos_i[:, 0], 7, None, ALU.logical_shift_right))
                ch.settle()
                ch.did(dve.tensor_copy(pos_hl[:], pos_i[:]))
                ch.settle()
                with dve.Fori(0, GROUPS // 2) as i:
                    for u in range(2):
                        g = i * 2 + u
                        at = bass.ds(g * GT, GT)

                        def place(part, n):
                            v = pos_hl[:, part].rearrange("p (k t) -> p k t", k=TOPK)[:, :, at]
                            return v.unsqueeze(3).broadcast_to([P, TOPK, GT, n])

                        def count(n):
                            return C["iota"][:, 0:n].unsqueeze(1).unsqueeze(1).broadcast_to([P, TOPK, GT, n])

                        dve.wait_ge(hot_used[r], g + 1)
                        dve.tensor_tensor(hot_hi[:, u], count(ST), place(0, ST), ALU.is_equal).then_inc(hi_ready[r], 1)
                        dve.tensor_tensor(hot_lo[:, u], count(P), place(1, P), ALU.is_equal).then_inc(hot_ready[r], 1)
                dve.wait_ge(hot_used[r], GROUPS + 2)
                ch.did(dve.tensor_copy(entry_pt[:], bank[6][:, 0:2 * ST]))
                ch.settle()
                ch.did(dve.scalar_tensor_tensor(entry_i[:], entry_pt[:, ST:2 * ST], float(TOPK * P), entry_pt[:, 0:ST],
                                                ALU.mult, ALU.add))
                ch.settle()
                dve.tensor_scalar(token_i[:], entry_i[:], 1, None, ALU.logical_shift_right)\
                    .then_inc(index_made[r], 1)

                def columns(G, k):
                    hold(ys_free[r], G + 1)
                    dve.tensor_copy(tcol[:, k], token_i[:, bass.ds(G * SGT, SGT)])
                    dve.tensor_copy(ecol[:, k], entry_i[:, bass.ds(G * SGT, SGT)]).then_inc(columns_ready[r], 1)

                dve.wait_ge(index_made[r], 1)
                for k in range(2):
                    columns(k, k)
                dve.wait_ge(we_ready[r], 1)
                ch.did(dve.tensor_scalar(den[:], wts[:, 1], 1.0, None, ALU.add))
                ch.settle()
                ch.did(dve.reciprocal(wts[:, 0], den[:]))
                ch.settle()
                ch.did(dve.tensor_tensor(wts[:, 1], wts[:, 1], wts[:, 0], ALU.mult))

                def copy_x(G, u):
                    dve.wait_ge(xgT_ready[r], G + 5)
                    dve.tensor_copy(xs[:, u], bank[0]).then_inc(xs_ready[r], 1)

                def copy_y(G, k):
                    dve.wait_ge(ys_free[r], G + 1)
                    dve.wait_ge(y_ready[r], G + 1)
                    dve.tensor_copy(ys[:, k].rearrange("p a d -> p (a d)"), bank[5 + k % 2]).then_inc(ys_ready[r], 1)

                copy_x(0, 0)

                def turn(i, last):
                    for k in range(4):
                        G = i * 4 + k
                        if not (last and k >= 2):
                            columns(G + 2, (k + 2) % 4)
                        if not (last and k == 3):
                            copy_x(G + 1, (k + 1) % 2)
                        copy_y(G, k)

                with dve.Fori(0, SGROUPS // 4 - 1) as i:
                    turn(i, False)
                turn(SGROUPS // 4 - 1, True)

                ch = new_chain()

                def combine(g, u):
                    if have(g, 0):
                        dve.wait_ge(share_added[r], g + 3)
                        dve.wait_ge(yb_ready[r], g + 1)
                        for j in range(GT):
                            xt = flat(x[:, tile(g * GT + j), :])
                            ins = dve.scalar_tensor_tensor(xt, flat(yb[:, tile(g), j, D:2 * D]), wts[:, 1, tile(g * GT + j)],
                                                           xt, ALU.mult, ALU.add)
                        ins.then_inc(x_done[r], 1)
                    if have(g, 1) and r == 1:
                        group_stats(g - 1, x_done[r], g, ch.sem)

                by_group(dve, combine, 1 if r == 1 else 0)
                ch.after(GROUPS, 1)
                dve.wait_ge(x_done[r], GROUPS)
                return ch

            ch = ffn(1, ch)

            make_rstd(ch)
            def rotate(G, u):
                if not isinstance(G, int) or G > 0:
                    dve.wait_ge(qk_ready, G * 2)
                for m, (cos, sin) in enumerate((("cosq", "sinq"), ("cosk", "sink"))):
                    for c, tab in enumerate((cos, sin)):
                        dve.wait_ge(proj_ready, G * 4 + 2 * m + c + 1)
                        dve.tensor_tensor(rot[:, m, c], bank[2 + 2 * m + c], C[tab][:], ALU.mult).then_inc(rot_ready, 1)
                dve.wait_ge(part3, G * 2 + 2)
                for m in range(2):
                    dve.wait_ge(rot_ready, G * 4 + 2 * m + 6)
                    dve.tensor_tensor(qk[:, u, m], rot[:, m, 0], rot[:, m, 1], ALU.add).then_inc(qk_ready, 1)
                x_G = x[:, bass.ds(G * GT, GT), :]
                dve.wait_ge(xn_ready[2], G + 1)
                dve.tensor_tensor(x_G, x_G, bo[:].unsqueeze(1).broadcast_to([P, GT, D]), ALU.add).then_inc(bo_added, 1)

            dve.sem_inc(rot_ready, 4)
            norm(2, rotate, 1)

            def softmax(g, s):
                par = s % 2
                sc = ps_s[par][:].rearrange("p (k w j) -> p k w j", w=2, j=P)
                for half in range(2):
                    hold(s_ready, g * (2 * STEPS) + (2 * s + half + 1))
                    pair = sc[:, 2 * half:2 * half + 2]
                    dve.copy_predicated(pair[:, :, 0, :], causal[:].unsqueeze(1).broadcast_to([P, 2, P]), pair[:, :, 1, :])\
                        .then_inc(merged, 1)
                for half in range(2):
                    dve.wait_ge(merged, g * (2 * STEPS) + (2 * s + half + 1))
                    dve.tensor_reduce(nm[:, par, 2 * half:2 * half + 2], sc[:, 2 * half:2 * half + 2, 0, :], AX_X, ALU.max,
                                      negate=True).then_inc(nm_ready, 1)

            def take_out(g, j):
                dve.wait_ge(pv_done, (g * GT + j + 3) * NQUAD)
                dve.tensor_copy(oS[:, j % 2], bank[6 + j % 2]).then_inc(oS_ready, 1)

            def normalise(g, j):
                o = bank[6 + j % 2].rearrange("p (h c) -> p h c", c=VC)
                dve.wait_ge(oq_ready, g * GT + j + 1)
                dve.reciprocal(rden[:, j % 2].unsqueeze(2), o[:, :, HDB:VW]).then_inc(rden_ready, 1)
                dve.wait_ge(rden_ready, g * GT + j + 1)
                dve.tensor_tensor(ob[:, j % 2].rearrange("p (h c) -> p h c", c=HDB), o[:, :, 0:HDB],
                                  rden[:, j % 2].unsqueeze(2).broadcast_to([P, HB, HDB]), ALU.mult).then_inc(o_ready, 1)

            def add_out(g, j):
                t = g * GT + j
                dve.wait_ge(wo_done, t + 1)
                dve.tensor_tensor(flat(x[:, tile(t), :]), flat(x[:, tile(t), :]), bank[6 + j % 2][:, P:2 * P], ALU.add)\
                    .then_inc(x_added, 1)

            ch = new_chain()

            def tile_stats(g, j):
                t = g * GT + j
                hold(x_added, t + 3)
                dve.bn_stats(flat(stat6[:, tile(t), :]), flat(x[:, tile(t), :])).then_inc(ch.sem, 1)

            def slot(g, s):
                for lag, do in ((TAKE_LAG, take_out), (NORM_LAG, normalise), (ADD_LAG, add_out), (STATS_LAG, tile_stats)):
                    g0, s0, there = step_at(g, s, lag)
                    if there and s0 % NQUAD == 0:
                        do(g0, s0 // NQUAD)
                g0, s0, there = step_at(g, s, 0)
                if there:
                    softmax(g0, s0)

            dve.wait_ge(bo_added, GROUPS)
            slots(dve, slot)
            dve.wait_ge(x_added, TILES + 2)
            ch.after(TILES, 1)
            ffn(3, ch)

        @block.tensor
        def _(pe):
            ident = C["ident"]
            pe.wait_ge(const_in, 16 * NCONST)
            pe.wait_ge(consts_made, 9)

            def transposed(r, g, u):
                if later(g):
                    pe.wait_ge(xnT_ready[r], g - 1)
                pe.wait_ge(xn_ready[r], g + 1)
                for j in range(GT):
                    ins = pe.transpose(bank[u][:, j * P:(j + 1) * P], xn[:, u, j, :], ident[:])
                ins.then_inc(xT_ready[r], 1)

            pe.sem_inc(xT_ready[0], 2)
            pe.sem_inc(fr_ready, 2)
            pe.matmul(bank[4][0:HAB, :], zeros[:, 0:HAB], zeros[:, :], start=True, stop=True)
            pe.sem_inc(sr_done, 2)

            def additive(g, u):
                if have(g, 0):
                    transposed(0, g, u)
                if have(g, 3):
                    pe.wait_ge(attb_ready, g - 2)
                    pe.wait_ge(leaky_ready, g - 2)
                    pe.matmul(bank[4][0:HAB, :], attb[:, 1 - u], leaky[:, 1 - u], start=False, stop=True,
                              skip_group_check=True).then_inc(sr_done, 1)
                if have(g, 1):
                    pe.wait_ge(xnT_ready[0], g)
                    pe.matmul(bank[2 + (1 - u)], W["WrT"][:], xnT[:, 1 - u], start=True, stop=True).then_inc(fr_ready, 1)

            by_group(pe, additive, 3, first=4)
            pe.wait_ge(a_dve, 2)
            for j in range(GT):
                ins = pe.transpose(bank[5][:, j * HAB:(j + 1) * HAB], pa[0:HAB, j * P:(j + 1) * P], ident[0:HAB, 0:HAB])
            ins.then_inc(a_pe, 1)
            pe.wait_ge(a_act, 2)
            pe.wait_ge(h_kept[0], GROUPS)
            for half in range(2):
                for j in range(GT):
                    for b4 in range(P // VC):
                        b = half * (P // VC) + b4
                        cols = j * HAB + b * HA
                        ins = pe.matmul(bank[6][b4 * VC:(b4 + 1) * VC, half * D:(half + 1) * D], paT[:, cols:cols + VC],
                                        h[:, b * GT + j, :], start=(j == 0), stop=(j == GT - 1),
                                        tile_position=(0, b4 * VC))
            ins.then_inc(a_pe, 1)
            pe.wait_ge(a_act, 3)
            for half in range(2):
                ins = pe.transpose(bank[5][:, half * P:(half + 1) * P], G_sb[:, half, :], ident[:])
            ins.then_inc(a_pe, 1)
            pe.wait_ge(a_act, 4)
            pe.matmul(bank[7][:, 0:HAB], W["WrT"][:], GT_sb[:], start=True, stop=True).then_inc(a_pe, 1)
            pe.wait_ge(a_dve, 3)
            for b in range(GROUPS):
                ins = pe.matmul(bank[b // GT][:, b % GT * D:(b % GT + 1) * D], ctxT[:, b:b + 1].broadcast_to([P, P]),
                                W["WfT"][:], start=True, stop=True)
                if b % GT == GT - 1:
                    ins.then_inc(a_pe, 1)

            def ffn(r):
                pe.sem_inc(xT_ready[r], 2)
                pe.sem_inc(lg_ready[r], 2)
                pe.sem_inc(lg_read[r], 2)

                def logits(g, u):
                    if have(g, 2):
                        pe.wait_ge(xnT_ready[r], g - 1)
                        pe.wait_ge(lg_read[r], g - 1)
                        for j in range(GT):
                            ins = pe.matmul(bank[2 + u][:, j * P:(j + 1) * P], xnT[:, u, j * P:(j + 1) * P],
                                            rwT[:], start=True, stop=True)
                        ins.then_inc(lg_ready[r], 1)
                    if have(g, 0):
                        transposed(r, g, u)

                by_group(pe, logits, 2)
                pe.wait_ge(took_ready[r], 1)
                pe.matmul(bank[4][:, 0:TILES * E], before_bf[:], took[:], start=True, stop=True)
                pe.matmul(bank[5][:, 0:TILES * E].rearrange("p (e t) -> p e t", e=E), ones_bf[:],
                          took[:].rearrange("p (t e) -> p e t", e=E), start=True, stop=True).then_inc(rank_ready[r], 1)
                pe.matmul(bank[6][:, 0:2 * ST], zeros[:, 0:P], zeros[:, 0:2 * ST], start=True, stop=True)
                pe.sem_inc(hot_used[r], 2)
                with pe.Fori(0, GROUPS // 2) as i:
                    for u in range(2):
                        g = i * 2 + u
                        for s in (hot_ready[r], en_ready[r], ent_ready[r]):
                            pe.wait_ge(s, g + 1)
                        for c in range(TOPK):
                            for j in range(GT):
                                ins = pe.matmul(bank[6][:, 0:2 * ST], hot_lo[:, u, c, j],
                                                hot_en[:, u, c, j].rearrange("p a b -> p (a b)"),
                                                start=False, stop=True, skip_group_check=True)
                        ins.then_inc(hot_used[r], 1)

                def turn_tokens(i, k):
                    pe.wait_ge(g_in[r][k], i * (16 * SGT) + 16 * SGT)
                    for j in range(SGT):
                        ins = pe.transpose(bank[0][:, j * P:(j + 1) * P], xg[:, k, j, :], ident[:])
                    ins.then_inc(xgT_ready[r], 1)

                pe.sem_inc(xgT_ready[r], 4)
                turn_tokens(0, 0)

                def turn(i, last):
                    for k in range(4):
                        G, u = i * 4 + k, k // 2
                        if k % 2 == 0:
                            pe.wait_ge(w_in[u], i * 32 + (32 + (r // 2) * (E // 2) * 32))
                        pe.wait_ge(xs_ready[r], G + 1)
                        for c in range(FC):
                            pe.matmul(bank[1 + c], w1b[:, u, c * P:(c + 1) * P], xs[:, k % 2], start=True, stop=True)\
                                .then_inc(h_ready[r], 1)
                        if not (last and k == 3):
                            turn_tokens(i + (k + 1) // 4, (k + 1) % 4)
                        for j in range(SGT):
                            for c in range(FC):
                                if j == 0:
                                    pe.wait_ge(gelu_done[r], G * FC + (c + 1))
                                ins = pe.matmul(bank[5 + k % 2][:, j * D:(j + 1) * D], hid[:, c, j * P:(j + 1) * P],
                                                w2b[:, u, c, :], start=(c == 0), stop=(c == FC - 1))
                        ins.then_inc(y_ready[r], 1)

                with pe.Fori(0, SGROUPS // 4 - 1) as i:
                    turn(i, False)
                turn(SGROUPS // 4 - 1, True)

            ffn(1)

            pe.sem_inc(xT_ready[2], 2)
            pe.sem_inc(v_ready, 2)

            def projections(g, u):
                if have(g, 1):
                    G, v = g - 1, 1 - u
                    pe.wait_ge(xnT_ready[2], g)
                    for m, k in enumerate(("WqT", "WqrT", "WkT", "WkrT")):
                        pe.wait_ge(rot_ready, G * 4 + m + 1)
                        pe.matmul(bank[2 + m], W[k][:], xnT[:, v], start=True, stop=True).then_inc(proj_ready, 1)
                if have(g, 0):
                    transposed(2, g, u)
                if have(g, 1):
                    pe.wait_ge(v_copied, G + 1)
                    for j in range(GT):
                        ins = pe.matmul(bank[6 + v][:, j * D:(j + 1) * D], xnT[:, v, j * P:(j + 1) * P], W["WvT"][:],
                                        start=True, stop=True)
                    ins.then_inc(v_ready, 1)

            by_group(pe, projections, 1)

            def scores(g, s):
                j, q = divmod(s, NQUAD)
                if q == 0:
                    pe.wait_ge(qk_in[j], g * (16 * (PARTS + 1)) + 16 * (PARTS + 1))
                for k in range(QUAD):
                    if k % 2 == 0 and (not isinstance(g, int) or g * STEPS + s >= 2):
                        pe.wait_ge(p_ready, g * (2 * STEPS) + (2 * s + k // 2 - 3))
                    hc = slice((q * QUAD + k) * P, (q * QUAD + k + 1) * P)
                    ins = pe.matmul(ps_s[s % 2][:, 2 * k * P:(2 * k + 2) * P].rearrange("p (w j) -> p w j", j=P),
                                    qb[0:KR1, j, hc], kb[0:KR1, j:j + 2, hc], start=True, stop=True)
                    if k % 2 == 1:
                        ins.then_inc(s_ready, 1)

            def turn_weights(g, s):
                if not isinstance(g, int) or g * STEPS + s >= 2:
                    pe.wait_ge(pT_copied, g * STEPS + (s - 1))
                pe.wait_ge(p_ready, g * (2 * STEPS) + (2 * s + 2))
                for k in range(QUAD):
                    ins = pe.transpose(bank[4 + s % 2][:, k * P:(k + 1) * P], pb[:, s % LANES, k, :], ident[:])
                ins.then_inc(pT_ready, 1)

            def weigh(g, s):
                j, q = divmod(s, NQUAD)
                if q == 0:
                    pe.wait_ge(vt_ready, (g * GT + j) * 2 + 2)
                    pe.wait_ge(x_added, g * GT + j + 1)
                pe.wait_ge(pTc_ready, g * STEPS + s + 1)
                for share, v in ((pT, vp), (pTc, vd)):
                    for k in range(QUAD):
                        ins = pe.matmul(bank[6 + j % 2][k * VC:(k + 1) * VC, q * P:(q + 1) * P],
                                        v[:, j % 2, q * QUAD + k, :], share[:, s % LANES, k * P:(k + 1) * P],
                                        start=share is pT, stop=share is pTc, tile_position=(0, k * VC))
                ins.then_inc(pv_done, 1)

            def turn_results(g, j):
                pe.wait_ge(oS_ready, g * GT + j + 1)
                for q in range(NQUAD):
                    ins = pe.transpose(bank[6 + j % 2][:, q * P:(q + 1) * P], oS[:, j % 2, q * P:(q + 1) * P], ident[:])
                ins.then_inc(oq_ready, 1)

            def turn_out(g, j):
                pe.wait_ge(o_ready, g * GT + j + 1)
                pe.transpose(bank[6 + j % 2][:, 0:P], ob[:, j % 2], ident[:]).then_inc(oT_ready, 1)

            def project(g, j):
                pe.wait_ge(oT_copied, g * GT + j + 1)
                pe.matmul(bank[6 + j % 2][:, P:2 * P], oT[:, j % 2], W["WoT"][:], start=True, stop=True).then_inc(wo_done, 1)

            pe.sem_inc(pv_done, 2 * NQUAD)
            pe.sem_inc(x_added, 2)
            pe.wait_ge(v_copied, GROUPS + 2)
            pe.wait_ge(rot_ready, 4 * GROUPS + 4)

            def slot(g, s):
                for lag, do in ((0, scores), (TURN_LAG, turn_weights), (WEIGH_LAG, weigh)):
                    g0, s0, there = step_at(g, s, lag)
                    if there:
                        do(g0, s0)
                for lag, do in ((TURN_RES_LAG, turn_results), (TURN_OUT_LAG, turn_out), (PROJ_LAG, project)):
                    g0, s0, there = step_at(g, s, lag)
                    if there and s0 % NQUAD == 0:
                        do(g0, s0 // NQUAD)

            slots(pe, slot)
            ffn(3)


def kernel(**inputs):
    import concourse.bacc as bacc
    from concourse.bass_utils import run_bass_kernel_spmd

    nc = bacc.Bacc("TRN2", target_bir_lowering=False, num_devices=1)
    i = {k: np.ascontiguousarray(v) for k, v in inputs.items()}
    rows = np.arange(D).reshape(HB, HDB)
    swap = rows.reshape(HB, 2, HDB // 2)[:, ::-1].reshape(HB, HDB).T.reshape(-1)
    rows = rows.T.reshape(-1)
    arrays = {
        "x": i["L0_attn_a_h"].reshape(B * N, D),
        "WrT": i["L0_attn_a_Wr"].T, "WfT": i["L0_attn_a_Wf"].T,
        "WqT": i["L0_attn_b_Wq"][rows].T, "WqrT": i["L0_attn_b_Wq"][swap].T,
        "WkT": i["L0_attn_b_Wk"][rows].T, "WkrT": i["L0_attn_b_Wk"][swap].T,
        "WvT": i["L0_attn_b_Wv"].T, "WoT": i["L0_attn_b_Wo"].T,
        "rwT": i["L0_ffn_router_w"].T,
        "attr": np.tile(i["L0_attn_a_att_r"].reshape(HDA), HA).reshape(D, 1),
        "gamma": i["L0_attn_a_ln_gamma"].reshape(1, D), "beta": i["L0_attn_a_ln_beta"].reshape(1, D),
        "bo": i["L0_attn_b_bo"].reshape(1, D),
        "w1": i["L0_ffn_w1"], "w2": i["L0_ffn_w2"],
    }
    arrays.update({"c_" + k: v for k, v in tables().items()})
    arrays = {"in_" + k: np.ascontiguousarray(v) for k, v in arrays.items()}
    aps = {k[3:]: nc.dram_tensor(k, v.shape, mybir.dt.from_np(v.dtype), kind="ExternalInput").ap()
           for k, v in arrays.items()}
    out = nc.dram_tensor("out_dram", (B * N, D), F32, kind="ExternalOutput").ap()
    hybrid_block(nc, aps, out)
    r = run_bass_kernel_spmd(nc, [arrays], core_ids=[0])
    return r.results[0]["out_dram"].reshape(B, N, D)
```
